# Optimizing a Trainium2 kernel written in Bass

```python
import numpy as np
import jax
import jax.numpy as jnp

def _softmax(x, axis=-1):
    return jax.nn.softmax(x, axis=axis)

def _gelu(x):
    return jax.nn.gelu(x, approximate=True)

def _silu(x):
    return jax.nn.silu(x)

def _sigmoid(x):
    return jax.nn.sigmoid(x)

def _layernorm(x, axis=-1, eps=1e-05):
    m = jnp.mean(x, axis=axis, keepdims=True)
    v = jnp.var(x, axis=axis, keepdims=True)
    return (x - m) / jnp.sqrt(v + eps)

def _scatter_add(tgt, idx, src, axis=0):
    return tgt.at[idx].add(src)

def _segment_sum(src, seg, n):
    return jax.ops.segment_sum(src, seg, n)
kernel_name = 'mk_gnn_preln_d2_gnn_r32_4285ae'

def setup_inputs(seed: int=0):
    np.random.seed(seed)
    _w = jnp.asarray

    def _rec_inputs():
        import jax
        import jax.numpy as jnp
        _gk = jax.random.key(seed)
        x = -0.0002117 + 1 * jax.random.normal(jax.random.fold_in(_gk, 1), (3125, 256), jnp.float32)
        src = jax.random.randint(jax.random.fold_in(_gk, 2), (50000,), 0, 3125, jnp.int32)
        dst = jnp.minimum((3125 * jax.random.uniform(jax.random.fold_in(_gk, 3), (50000,)) ** 2.0).astype(jnp.int32), 99999)
        _o = jnp.argsort(dst, stable=True)
        src = src[_o]
        dst = dst[_o]
        edge_type_8 = jax.random.randint(jax.random.fold_in(_gk, 13), (50000,), 0, 8, jnp.int32)
        edge_weight = jax.random.uniform(jax.random.fold_in(_gk, 14), (50000,), jnp.float32, 0.0, 1)
        return (x, src, dst, edge_type_8, edge_weight)
    x, src, dst, edge_type_8, edge_weight = _rec_inputs()

    def _L0_gnn_setup():
        import jax, jax.numpy as jnp
        import numpy as np
        N_NODES = 3125
        N_EDGES = 100000
        D_IN = 256
        D_OUT = 256
        key = jax.random.key(seed)
        k1, k2, k3, k4, k5, k6 = jax.random.split(key, 6)
        x = jax.random.normal(k1, (N_NODES, D_IN), dtype=jnp.float32)
        edge_src = jax.random.randint(k2, (N_EDGES,), 0, N_NODES, dtype=jnp.int32)
        edge_dst = jax.random.randint(k3, (N_EDGES,), 0, N_NODES, dtype=jnp.int32)
        edge_weight = jax.random.uniform(k4, (N_EDGES,), dtype=jnp.float32)
        weight = jax.random.normal(k5, (D_IN, D_OUT), dtype=jnp.float32) * 0.02
        bias = jax.random.uniform(k6, (D_OUT,), dtype=jnp.float32)
        return {'x': x, 'edge_src': edge_src, 'edge_dst': edge_dst, 'edge_weight': edge_weight, 'weight': weight, 'bias': bias}
    _L0_gnn_all = _L0_gnn_setup()
    _L0_gnn_in = {k: v for k, v in _L0_gnn_all.items() if k in ('weight', 'bias')}
    del _L0_gnn_all

    def _L1_gnn_setup():
        import jax, jax.numpy as jnp
        import numpy as np
        N_NODES = 50000
        N_EDGES = 25000
        D_IN = 256
        D_OUT = 256
        N_REL = 8
        key = jax.random.key(seed)
        k_x, k_ei, k_et, k_w = jax.random.split(key, 4)
        x = jax.random.normal(k_x, (N_NODES, D_IN), dtype=jnp.float32)
        edge_index = jax.random.randint(k_ei, (2, N_EDGES), 0, N_NODES, dtype=jnp.int32)
        edge_type = jax.random.randint(k_et, (N_EDGES,), 0, N_REL, dtype=jnp.int32)
        limit = float(np.sqrt(6.0 / (D_IN + D_OUT)))
        weight = jax.random.uniform(k_w, (N_REL, D_IN, D_OUT), dtype=jnp.float32, minval=-limit, maxval=limit)
        bias = jnp.zeros((D_OUT,), dtype=jnp.float32)
        return {'x': x, 'edge_index': edge_index, 'edge_type': edge_type, 'weight': weight, 'bias': bias}
    _L1_gnn_all = _L1_gnn_setup()
    _L1_gnn_in = {k: v for k, v in _L1_gnn_all.items() if k in ('weight', 'bias')}
    del _L1_gnn_all
    return {'x': x, 'src': src, 'dst': dst, 'edge_type_8': edge_type_8, 'edge_weight': edge_weight, 'L0_gnn_weight': _L0_gnn_in['weight'], 'L0_gnn_bias': _L0_gnn_in['bias'], 'L1_gnn_weight': _L1_gnn_in['weight'], 'L1_gnn_bias': _L1_gnn_in['bias']}

def reference(x, src, dst, edge_type_8, edge_weight, L0_gnn_weight, L0_gnn_bias, L1_gnn_weight, L1_gnn_bias):
    import jax
    import jax.numpy as jnp

    def _L0_gnn_ref(x, edge_src, edge_dst, edge_weight, weight, bias):
        import jax, jax.numpy as jnp
        import numpy as np
        N_NODES = 3125
        N_EDGES = 100000
        D_IN = 256
        D_OUT = 256
        support = x @ weight
        msgs = support[edge_src] * edge_weight[:, None]
        out = jax.ops.segment_sum(msgs, edge_dst, num_segments=N_NODES)
        return out + bias

    def _L1_gnn_ref(x, edge_index, edge_type, weight, bias):
        import jax, jax.numpy as jnp
        import numpy as np
        N_NODES = 50000
        N_EDGES = 25000
        D_IN = 256
        D_OUT = 256
        N_REL = 8
        num_nodes = x.shape[0]
        row, col = (edge_index[0], edge_index[1])
        xt = jnp.einsum('ni,rio->rno', x, weight)
        messages = xt[edge_type, col]
        out = jax.ops.segment_sum(messages, row, num_segments=num_nodes)
        return jax.nn.relu(out + bias)
    edge_index = jnp.stack([src, dst])
    h = jnp.maximum(_layernorm(x, axis=-1), 0.0)
    x = x + _L0_gnn_ref(h, src, dst, edge_weight, L0_gnn_weight, L0_gnn_bias)
    h = jnp.maximum(_layernorm(x, axis=-1), 0.0)
    x = x + _L1_gnn_ref(h, edge_index, edge_type_8, L1_gnn_weight, L1_gnn_bias)
    return x

_drawn_inputs = setup_inputs


def setup_inputs(seed=0):
    import zlib

    import numpy as np

    out = dict(_drawn_inputs(seed))
    spreads = {'L1_gnn_bias': (0.0, 0.466)}
    factors = {}
    for name, (base, spread) in spreads.items():
        noise = np.random.default_rng([zlib.crc32(name.encode()), seed]).standard_normal(out[name].shape)
        drawn = base * np.exp(spread * noise) if base else spread * noise
        out[name] = jnp.asarray(drawn.astype(out[name].dtype))
    for name, factor in factors.items():
        out[name] = (out[name] * factor).astype(out[name].dtype)
    return out
```

```python
import concourse.bass as bass
from concourse import mybir
from contextlib import ExitStack


def gnn_kernel(nc, x, src, dst, etype, ew, w0, b0, w1, b1, out):
    f32, i32 = mybir.dt.float32, mybir.dt.int32
    bf16, f16 = mybir.dt.bfloat16, mybir.dt.float16
    ALU = mybir.AluOpType
    ACT = mybir.ActivationFunctionType
    AX = mybir.AxisListType
    ds = bass.ds

    P = 128
    N, D = x.shape
    E = src.shape[0]
    R = w1.shape[0]
    KC = D // P
    NB = -(-N // P)
    NFULL = N // P
    NREST = N - NFULL * P
    NP = NB * P
    EP = 125
    EC = E // EP
    T = -(-E // P) + NB
    U = 16
    AHEAD = 8
    TI = T // U
    CI = EC // U
    assert EP * EC == E and TI * U == T and CI * U == EC and CI == NB and TI == CI + 1
    TU = 5
    assert NB % TU == 0 and D == KC * P and P == 128
    SR = 4
    NSF = (5, 2)
    EPS = 1e-5
    KEY_LOW = 16

    table0 = nc.dram_tensor("table0", [NP, D], f32, kind="Internal").ap()
    table1 = nc.dram_tensor("table1", [R * NP, D], f32, kind="Internal").ap()
    tables = (table0, table1)

    ctx = ExitStack()
    with ctx:
        def sb(name, shape, dt=f32):
            return ctx.enter_context(nc.sbuf_tensor(name, shape, dt))

        def sem(name):
            return ctx.enter_context(nc.semaphore(name))

        iota_p = sb("iota_p", [P, P])
        iota_p16 = sb("iota_p16", [P, P], f16)
        iota_t16 = sb("iota_t16", [P, T], f16)
        part = sb("part", [P, 1])
        ident = sb("ident", [P, P])
        before = sb("before", [P, P])
        upto = sb("upto", [P, P])
        ones = sb("ones", [P, P])
        zeros16 = sb("zeros16", [P, T], bf16)
        bias0 = sb("bias0", [P, D])
        bias1 = sb("bias1", [P, D])
        w0_sb = sb("w0_sb", [P, KC, D])
        x_sb = sb("x_sb", [P, NB, D])
        x1_sb = sb("x1_sb", [P, NB, D])
        agg1 = x_sb
        st_sum = sb("st_sum", [P, NB])
        st_sq = sb("st_sq", [P, NB])
        st_mean = sb("st_mean", [P, NB])
        st_std = sb("st_std", [P, NB])
        rstd = sb("rstd", [P, NB])
        shift = sb("shift", [P, NB])
        bn6 = sb("bn6", [P, NB, 6])
        eps_t = sb("eps_t", [P, 1])
        h_ring = sb("h_ring", [P, TU, D])
        hT_ring = sb("hT_ring", [P, TU, KC, P])
        row_stage0 = x1_sb[:, 0:TU, :]
        src_i = sb("src_i", [EP, EC], i32)
        dst_i = sb("dst_i", [EP, EC], i32)
        type_i = sb("type_i", [EP, EC], i32)
        ew_f = sb("ew_f", [EP, EC])
        ew_r = [ew_f, sb("ew_r1", [EP, EC]), sb("ew_r2", [EP, EC])]
        tmp_b = sb("tmp_b", [EP, EC], bf16)
        tmp_i = sb("tmp_i", [EP, EC], i32)
        tmp_f = sb("tmp_f", [EP, EC])
        row_f = sb("row_f", [EP, EC])
        bucket = sb("bucket", [EP, EC], f16)
        key_hi = [sb(f"key_hi{i}", [EP, EC]) for i in range(2)]
        key_lo = [sb(f"key_lo{i}", [EP, EC]) for i in range(2)]
        pos_t = [sb(f"pos_t{i}", [EP, EC]) for i in range(2)]
        pos_p = [sb(f"pos_p{i}", [EP, EC]) for i in range(2)]
        mask_mem = sb("mask_mem", [P, NB * EC], bf16)
        mask = mask_mem[0:EP, :].rearrange("p (b c) -> p b c", b=NB)
        w1_sb = mask_mem[:, 0:2 * KC * R * D].bitcast(f32).rearrange("p (k r d) -> p k r d", k=KC, r=R)
        scan = sb("scan", [P, P * 80])
        scan3 = scan[0:EP, 0:NB * EC].rearrange("p (b c) -> p b c", b=NB)
        stage1 = scan[:, 0:TU * R * D].rearrange("p (u r d) -> p u r d", u=TU, r=R)
        row_tot = sb("row_tot", [EP, NB])
        tot_i = sb("tot_i", [P, NB], i32)
        tiles_f = sb("tiles_f", [P, NB])
        tile_end = sb("tile_end", [P, NB])
        offs = sb("offs", [P, NB])
        col_i = sb("col_i", [NB, 1], i32)
        col_f = sb("col_f", [NB, 1])
        col_end = sb("col_end", [NB, 1])
        ended = sb("ended", [NB, T])
        tile_row = sb("tile_row", [1, T])
        tile_off = [sb(f"tile_off{i}", [1, T], i32) for i in range(2)]
        oh_t = sb("oh_t", [EP, SR, T], bf16)
        oh_f = [sb(f"oh_f{k}", [EP, SR, P], f16 if k < 2 else bf16) for k in range(5)]
        idx = sb("idx", [P, T], i32)
        local = sb("local", [P, T])
        ew_s = sb("ew_s", [P, T])
        idx_ring = sb("idx_ring", [P, U], i32)
        rows = sb("rows", [P, U, D])
        oh_m = sb("oh_m", [P, U, P])
        scratch = oh_m[:, :, :].rearrange("p u m -> p (u m)")
        dec_i, dec_j = (scratch[:, k * T:(k + 1) * T].bitcast(i32) for k in (0, 1))
        dec_f, dec_g = (scratch[:, k * T:(k + 1) * T] for k in (2, 3))

        bank = [ctx.enter_context(nc.psum_tensor(f"bank{i}", [P, 512], f32)) for i in range(8)]

        def transposed(u):
            return bank[(0, 1, 2, 5, 6)[u]][:, 0:D].rearrange("p (k n) -> p k n", k=KC)

        def table_bank(g):
            return bank[3 + g % 2]
        RANK = bank[7]
        MSG0, MSGN = 2, 4
        G1 = R // 2
        assert G1 == 4

        s_const = sem("s_const")
        s_ident = sem("s_ident")
        s_edges = sem("s_edges")
        s_x = sem("s_x")
        s_w = sem("s_w")
        s_bias = sem("s_bias")
        s_dve = sem("s_dve")
        s_act = sem("s_act")
        s_mask = sem("s_mask")
        s_scan = sem("s_scan")
        s_rowtot = [sem(f"s_rowtot{i}") for i in range(2)]
        s_total = [sem(f"s_total{i}") for i in range(2)]
        s_colend = [sem(f"s_colend{i}") for i in range(2)]
        s_colcum = [sem(f"s_colcum{i}") for i in range(2)]
        s_ended = [sem(f"s_ended{i}") for i in range(2)]
        s_tilerow = [sem(f"s_tilerow{i}") for i in range(2)]
        s_sortready = sem("s_sortready")
        s_sortfree = sem("s_sortfree")
        s_sorted = [sem(f"s_sorted{i}") for i in range(2)]
        s_decoded = [sem(f"s_decoded{i}") for i in range(2)]
        s_stats = [sem(f"s_stats{i}") for i in range(2)]
        s_std = [sem(f"s_std{i}") for i in range(2)]
        s_norm = [sem(f"s_norm{i}") for i in range(2)]
        s_h = [sem(f"s_h{i}") for i in range(2)]
        s_tp = [sem(f"s_tp{i}") for i in range(2)]
        s_hT = [sem(f"s_hT{i}") for i in range(2)]
        s_mm = [sem(f"s_mm{i}") for i in range(2)]
        s_staged = [sem(f"s_staged{i}") for i in range(2)]
        s_stored = [[sem(f"s_stored{i}_{u}") for u in range(TU)] for i in range(2)]
        s_bankfree = [sem(f"s_bankfree{i}") for i in range(2)]
        s_agg = [sem(f"s_agg{i}") for i in range(2)]
        s_idx = sem("s_idx")
        s_gather = [sem(f"s_gather{u}") for u in range(U)]
        s_ohm = sem("s_ohm")
        s_msg = sem("s_msg")
        s_acc = sem("s_acc")
        s_final = sem("s_final")
        s_out = sem("s_out")
        s_place = sem("s_place")

        block = ctx.enter_context(nc.Block())

        @block.sync
        def _(sp):
            def edges(a):
                return a.rearrange("(p c) -> p c", p=EP)
            sp.dma_start(dst_i[:, :], edges(dst)).then_inc(s_edges, 16)
            sp.dma_start(src_i[:, :], edges(src)).then_inc(s_edges, 16)
            sp.dma_start(type_i[:, :], edges(etype)).then_inc(s_edges, 16)
            sp.dma_start(ew_f[:, :], edges(ew)).then_inc(s_edges, 16)
            sp.wait_ge(s_const, 2)
            sp.dma_start(x_sb[0:NREST, NFULL, :], x[NFULL * P:N, :]).then_inc(s_x, 16)
            sp.dma_start(x_sb[:, 0:NFULL, :],
                         x[0:NFULL * P, :].rearrange("(b p) d -> p b d", p=P)).then_inc(s_x, 16)
            sp.dma_start(w0_sb[:, :, :], w0.rearrange("(k p) d -> p k d", p=P)).then_inc(s_w, 16)
            sp.dma_start(bias0[:, :], b0.partition_broadcast(P)).then_inc(s_bias, 16)
            sp.dma_start(bias1[:, :], b1.partition_broadcast(P)).then_inc(s_bias, 16)
            for layer in range(2):
                if layer == 1:
                    sp.wait_ge(s_place, 1)
                    for k in range(KC):
                        sp.dma_start(w1_sb[:, k, :, :],
                                     w1[:, k * P:(k + 1) * P, :].rearrange("r p d -> p r d")).then_inc(s_w, 16)
                with sp.Fori(0, NB // TU) as i:
                    for u in range(TU):
                        if layer == 0:
                            sp.wait_ge(s_staged[0], i * TU + (u + 1))
                            sp.dma_start(table0[ds(i * (TU * P) + u * P, P), :],
                                         row_stage0[:, u, :]).then_inc(s_stored[0][u], 16)
                        else:
                            sp.wait_ge(s_bankfree[1], i * (TU * G1) + (u + 1) * G1)
                            tv = table1.rearrange("(r n) d -> n r d", r=R)
                            sp.dma_start(tv[ds(i * (TU * P) + u * P, P), :, :],
                                         stage1[:, u, :, :]).then_inc(s_stored[1][u], 16)
            sp.wait_ge(s_final, 1)
            sp.dma_start(out[0:NFULL * P, :].rearrange("(b p) d -> p b d", p=P),
                         x1_sb[:, 0:NFULL, :]).then_inc(s_out, 16)
            sp.dma_start(out[NFULL * P:N, :], x1_sb[0:NREST, NFULL, :]).then_inc(s_out, 16)
            sp.wait_ge(s_out, 32)

        @block.gpsimd
        def _(pool):
            allow = dict(allow_small_or_imprecise_dtypes=True)
            nc.gpsimd.iota(iota_p[:, :], pattern=[[1, P]], base=0, channel_multiplier=0, **allow)
            nc.gpsimd.iota(iota_p16[:, :], pattern=[[1, P]], base=0, channel_multiplier=0, **allow)
            nc.gpsimd.iota(iota_t16[:, :], pattern=[[1, T]], base=0, channel_multiplier=0, **allow)
            nc.gpsimd.iota(part[:, :], pattern=[[0, 1]], base=0, channel_multiplier=1, **allow)
            nc.gpsimd.memset(zeros16[:, :], 0.0)
            nc.gpsimd.memset(eps_t[:, :], EPS)
            nc.gpsimd.memset(ones[:, :], 1.0).then_inc(s_const, 1)
            nc.gpsimd.memset(x_sb[:, NFULL, :], 0.0).then_inc(s_const, 1)
            for layer in range(2):
                for u in range(TU):
                    pool.wait_ge(s_stored[layer][u], 16 * (NB // TU))
                with pool.Fori(0, TI) as i:
                    for u in range(U):
                        if u % AHEAD == 0:
                            pool.wait_ge(s_idx, i * (U // AHEAD) + (u // AHEAD + layer * (T // AHEAD) + 1))
                            pool.nop(nofuse=True)
                        pool.indirect_dma_start(
                            out=rows[:, u, :], out_offset=None, in_=tables[layer][:, :],
                            in_offset=bass.IndirectOffsetOnAxis(ap=idx_ring[:, u:u + 1], axis=0),
                        ).then_inc(s_gather[u], 16)

        @block.scalar
        def _(act):
            steps = [0]

            def step(ins):
                steps[0] += 1
                ins.then_inc(s_act, 1)
                act.wait_ge(s_act, steps[0])

            act.wait_ge(s_x, 32)
            act.wait_ge(s_const, 2)
            with act.Fori(0, NB) as b:
                nc.scalar.activation(x1_sb[:, ds(b, 1), :], x_sb[:, ds(b, 1), :], ACT.Identity, scale=-1.0 / D,
                                     accum_out=st_mean[:, ds(b, 1)]).then_inc(s_stats[0], 1)
            act.wait_ge(s_stats[0], NB)
            with act.Fori(0, NB) as b:
                nc.scalar.activation(x1_sb[:, ds(b, 1), :], x_sb[:, ds(b, 1), :], ACT.Square,
                                     bias=st_mean[:, ds(b, 1)],
                                     accum_out=st_sq[:, ds(b, 1)]).then_inc(s_stats[0], 1)
            act.wait_ge(s_stats[0], 2 * NB)
            nc.scalar.activation(st_std[:, :], st_sq[:, :], ACT.Sqrt, bias=eps_t[:, 0:1],
                                 scale=1.0 / D).then_inc(s_std[0], 1)

            for layer in range(2):
                xs = x_sb if layer == 0 else x1_sb
                if layer == 1:
                    act.wait_ge(s_stats[1], 1)
                    nc.scalar.activation(st_std[:, :], st_sq[:, :], ACT.Sqrt, bias=eps_t[:, 0:1],
                                         scale=1.0 / D).then_inc(s_std[1], 1)
                act.wait_ge(s_norm[layer], 1)
                for u in range(TU):
                    nc.scalar.activation(h_ring[:, u, :], xs[:, u, :], ACT.Relu, bias=shift[:, u:u + 1],
                                         scale=rstd[:, u:u + 1]).then_inc(s_h[layer], 1)

                def staged_group(i, first, last):
                    for u in range(TU):
                        n1 = i * TU + (u + 1)
                        act.wait_ge(s_tp[layer], n1)
                        nc.scalar.activation(hT_ring[:, u, :, :], transposed(u), ACT.Copy).then_inc(s_hT[layer], 1)
                        if not last:
                            b = i * TU + (u + TU)
                            nc.scalar.activation(h_ring[:, u, :], xs[:, ds(b, 1), :], ACT.Relu,
                                                 bias=shift[:, ds(b, 1)],
                                                 scale=rstd[:, ds(b, 1)]).then_inc(s_h[layer], 1)
                        if layer == 0:
                            act.wait_ge(s_mm[0], n1)
                            if not first:
                                act.wait_ge(s_stored[0][u], i * 16)
                            nc.scalar.activation(row_stage0[:, u, :], table_bank(u)[:, 0:D],
                                                 ACT.Copy).then_inc(s_staged[0], 1)

                staged_group(0, True, False)
                with act.Fori(1, NB // TU - 1) as i:
                    staged_group(i, False, False)
                staged_group(NB // TU - 1, False, True)

                act.wait_ge(s_decoded[layer], 1)
                for u in range(0, U, AHEAD):
                    if layer == 1:
                        act.wait_ge(s_msg, T)
                    nc.scalar.activation(idx_ring[:, u:u + AHEAD], idx[:, u:u + AHEAD],
                                         ACT.Copy).then_inc(s_idx, 1)
                with act.Fori(1, TI) as i:
                    for u in range(0, U, AHEAD):
                        act.wait_ge(s_msg, i * U + (u + AHEAD - U + layer * T))
                        nc.scalar.activation(idx_ring[:, u:u + AHEAD], idx[:, ds(i * U + u, AHEAD)],
                                             ACT.Copy).then_inc(s_idx, 1)

        @block.vector
        def _(dve):
            steps = [0]

            def step(ins):
                steps[0] += 1
                ins.then_inc(s_dve, 1)
                dve.wait_ge(s_dve, steps[0])

            V = nc.vector
            dve.sem_inc(s_acc, 1)
            dve.wait_ge(s_const, 1)
            V.tensor_scalar(before[:, :], iota_p[:, :], part[:, 0:1], None, ALU.is_gt)
            V.tensor_scalar(upto[:, :], iota_p[:, :], part[:, 0:1], None, ALU.is_ge)
            step(V.tensor_scalar(ident[:, :], iota_p[:, :], part[:, 0:1], None, ALU.is_equal))
            V.sem_inc(s_ident, 1)

            def keys(layer):
                node, other = (dst_i, src_i) if layer == 0 else (src_i, dst_i)
                step(V.tensor_scalar(tmp_i[:, :], node[:, :], 7, None, ALU.logical_shift_right))
                step(V.tensor_copy(bucket[:, :], tmp_i[:, :]))
                step(V.tensor_scalar(tmp_i[:, :], node[:, :], P - 1, None, ALU.bitwise_and))
                step(V.tensor_copy(key_lo[layer][:, :], tmp_i[:, :]))
                if layer == 0:
                    step(V.tensor_copy(row_f[:, :], other[:, :]))
                else:
                    step(V.tensor_copy(row_f[:, :], type_i[:, :]))
                    step(V.tensor_copy(tmp_f[:, :], other[:, :]))
                    step(V.scalar_tensor_tensor(row_f[:, :], row_f[:, :], float(NP), tmp_f[:, :],
                                                ALU.mult, ALU.add))
                step(V.tensor_copy(tmp_i[:, :], row_f[:, :]))
                step(V.tensor_scalar(tmp_i[:, :], tmp_i[:, :], 4, None, ALU.logical_shift_right))
                step(V.tensor_copy(key_hi[layer][:, :], tmp_i[:, :]))
                step(V.scalar_tensor_tensor(tmp_f[:, :], key_hi[layer][:, :], -float(KEY_LOW), row_f[:, :],
                                            ALU.mult, ALU.add))
                V.tensor_scalar(key_hi[layer][:, :], key_hi[layer][:, :], 1.0, None, ALU.add)
                step(V.scalar_tensor_tensor(key_lo[layer][:, :], tmp_f[:, :], float(P), key_lo[layer][:, :],
                                            ALU.mult, ALU.add))

            def masks(b):
                return V.tensor_scalar(mask[:, ds(b, 1), :], bucket[:, :], b_col(b), None, ALU.is_equal)

            def totals(layer):
                step(V.tensor_copy(row_tot[:, :], scan3[:, :, EC - 1]))
                V.sem_inc(s_rowtot[layer], 1)
                dve.wait_ge(s_total[layer], 1)
                step(V.tensor_scalar(tiles_f[:, :], RANK[:, 0:NB], float(P - 1), None, ALU.add))
                step(V.tensor_copy(tot_i[:, :], tiles_f[:, :]))
                step(V.tensor_scalar(tot_i[:, :], tot_i[:, :], 7, None, ALU.logical_shift_right))
                step(V.tensor_copy(tiles_f[:, :], tot_i[:, :]))
                step(V.tensor_tensor_scan(tile_end[:, :], tiles_f[:, :], tiles_f[:, :], 0.0,
                                          ALU.add, ALU.max))
                step(V.tensor_tensor(tile_end[:, :], tile_end[:, :], tiles_f[:, :], ALU.subtract))
                step(V.tensor_scalar(tile_end[:, :], tile_end[:, :], float(P), -1.0, ALU.mult, ALU.add))
                step(V.tensor_tensor(offs[0:EP, :], tile_end[0:EP, :], RANK[0:EP, 32:32 + NB], ALU.add))
                step(V.tensor_scalar(col_f[:, :], RANK[0:NB, 64:65], float(P - 1), None, ALU.add))
                step(V.tensor_copy(col_i[:, :], col_f[:, :]))
                step(V.tensor_scalar(col_i[:, :], col_i[:, :], 7, None, ALU.logical_shift_right))
                V.tensor_copy(col_f[:, :], col_i[:, :]).then_inc(s_colend[layer], 1)
                dve.wait_ge(s_colcum[layer], 1)
                step(V.tensor_copy(col_end[:, :], RANK[0:NB, 65:66]))
                V.tensor_scalar(ended[:, :], iota_t16[0:NB, :], col_end[:, 0:1], None,
                                ALU.is_ge).then_inc(s_ended[layer], 1)
                dve.wait_ge(s_tilerow[layer], 1)
                step(V.tensor_scalar(tile_row[:, :], RANK[0:1, 0:T], float(NB - 1), float(D),
                                     ALU.min, ALU.mult))
                step(V.tensor_copy(tile_off[layer][:, :], tile_row[:, :]))

            def place_block(b):
                return V.scalar_tensor_tensor(scan3[:, ds(b, 1), :], scan3[:, ds(b, 1), :], offs[0:EP, ds(b, 1)],
                                              mask[:, ds(b, 1), :], ALU.add, ALU.mult)

            def positions(layer):
                step(V.tensor_reduce(tmp_f[:, :], scan3.rearrange("p b c -> p c b"), AX.X, ALU.add))
                step(V.tensor_copy(tmp_i[:, :], tmp_f[:, :]))
                step(V.tensor_scalar(tmp_i[:, :], tmp_i[:, :], 7, None, ALU.logical_shift_right))
                step(V.tensor_copy(pos_t[layer][:, :], tmp_i[:, :]))
                step(V.scalar_tensor_tensor(pos_p[layer][:, :], pos_t[layer][:, :], -float(P), tmp_f[:, :],
                                            ALU.mult, ALU.add))

            b_tab = iota_p

            def b_col(b):
                return b_tab[0:EP, ds(b, 1)]

            def scan_block(b):
                m = mask[:, ds(b, 1), :].rearrange("p a c -> p (a c)")
                s = scan3[:, ds(b, 1), :].rearrange("p a c -> p (a c)")
                return V.tensor_tensor_scan(s, m, m, 0.0, ALU.add, ALU.max)

            def sort_tile(layer, c, u, n1):
                dve.wait_ge(s_sortfree, n1)
                s = u % SR
                V.tensor_scalar(oh_t[:, s, :], iota_t16[0:EP, :], pos_t[layer][:, ds(c, 1)], None, ALU.is_equal)
                fields = [key_hi[layer], key_lo[layer]] + (ew_r if layer == 0 else [])
                for k, f in enumerate(fields):
                    last = V.tensor_scalar(oh_f[k][:, s, :], iota_p16[0:EP, :], pos_p[layer][:, ds(c, 1)],
                                           f[:, ds(c, 1)], ALU.is_equal, ALU.mult)
                last.then_inc(s_sortready, 1)

            def decode(layer, bk):
                dve.wait_ge(s_sorted[layer], 1)
                step(V.tensor_copy(dec_i[:, :], bank[bk + 1][:, 0:T]))
                step(V.tensor_scalar(dec_j[:, :], dec_i[:, :], 7, None, ALU.logical_shift_right))
                step(V.tensor_copy(dec_f[:, :], dec_j[:, :]))
                step(V.tensor_scalar(dec_j[:, :], dec_i[:, :], P - 1, None, ALU.bitwise_and))
                step(V.tensor_copy(local[:, :], dec_j[:, :]))
                step(V.scalar_tensor_tensor(dec_f[:, :], bank[bk][:, 0:T], float(KEY_LOW), dec_f[:, :],
                                            ALU.mult, ALU.add))
                step(V.tensor_scalar(dec_f[:, :], dec_f[:, :], -float(KEY_LOW), 0.0, ALU.add, ALU.max))
                step(V.tensor_scalar(dec_g[:, :], bank[bk][:, 0:T], 0.0, -2.0 * P, ALU.is_equal, ALU.mult))
                step(V.tensor_tensor(local[:, :], local[:, :], dec_g[:, :], ALU.add))
                if layer == 0:
                    step(V.tensor_copy(dec_g[:, :], bank[bk + 2][:, 0:T]))
                    step(V.tensor_tensor(dec_g[:, :], dec_g[:, :], bank[bk + 3][:, 0:T], ALU.add))
                    step(V.tensor_tensor(ew_s[:, :], dec_g[:, :], bank[bk + 4][:, 0:T], ALU.add))
                step(V.tensor_copy(idx[:, :], dec_f[:, :]))
                V.sem_inc(s_decoded[layer], 1)

            dve.wait_ge(s_edges, 64)
            keys(0)
            step(V.tensor_copy(tmp_b[:, :], ew_f[:, :]))
            step(V.tensor_tensor(ew_r[1][:, :], ew_f[:, :], tmp_b[:, :], ALU.subtract))
            step(V.tensor_copy(tmp_b[:, :], ew_r[1][:, :]))
            step(V.tensor_tensor(ew_r[2][:, :], ew_r[1][:, :], tmp_b[:, :], ALU.subtract))
            with dve.Fori(0, NB) as b:
                masks(b).then_inc(s_mask, 1)
            dve.wait_ge(s_mask, NB)
            with dve.Fori(0, NB) as b:
                scan_block(b).then_inc(s_scan, 1)
            dve.wait_ge(s_scan, NB)
            totals(0)
            dve.wait_ge(s_std[0], 1)
            step(V.reciprocal(rstd[:, :], st_std[:, :]))
            step(V.tensor_tensor(shift[:, :], st_mean[:, :], rstd[:, :], ALU.mult))
            V.sem_inc(s_norm[0], 1)
            with dve.Fori(0, NB) as b:
                place_block(b).then_inc(s_scan, 1)
            dve.wait_ge(s_scan, 2 * NB)
            positions(0)
            keys(1)

            with dve.Fori(0, CI) as i:
                for u in range(U):
                    sort_tile(0, i * U + u, u, i * U + (u + 1))
                masks(i).then_inc(s_mask, 1)
                dve.wait_ge(s_mask, i + (NB + 1))
                scan_block(i).then_inc(s_scan, 1)
            dve.wait_ge(s_scan, 3 * NB)
            decode(0, 0)
            dve.wait_ge(s_x, 32)
            dve.wait_ge(s_bias, 32)
            for u in range(TU):
                dve.wait_ge(s_stored[0][u], 16 * (NB // TU))
            V.tensor_tensor(x1_sb[:, :, :], x_sb[:, :, :],
                            bias0[:, :].rearrange("p (b d) -> p b d", b=1).broadcast_to([P, NB, D]), ALU.add)
            for t in range(AHEAD):
                V.tensor_scalar(oh_m[:, t, :], iota_p[:, :], local[:, t:t + 1], ew_s[:, t:t + 1],
                                ALU.is_equal, ALU.mult).then_inc(s_ohm, 1)
            totals(1)
            with dve.Fori(0, NB) as b:
                place_block(b).then_inc(s_scan, 1)
            dve.wait_ge(s_scan, 4 * NB)
            V.sem_inc(s_place, 1)
            positions(1)

            def one_hot(layer, t, u):
                if layer == 0:
                    return V.tensor_scalar(oh_m[:, u, :], iota_p[:, :], local[:, ds(t, 1)], ew_s[:, ds(t, 1)],
                                           ALU.is_equal, ALU.mult)
                return V.tensor_scalar(oh_m[:, u, :], iota_p[:, :], local[:, ds(t, 1)], None, ALU.is_equal)

            def accumulate(layer, t, u, n):
                acc = (x1_sb if layer == 0 else agg1)[:, :, :].rearrange("p b d -> p (b d)")
                off = dve.value_load(tile_off[layer][0:1, ds(t, 1)], min_val=0, max_val=(NB - 1) * D)
                dve.wait_ge(s_msg, n + 1)
                dve.wait_ge(s_acc, n + 1)
                V.tensor_tensor(acc[:, ds(off, D)], acc[:, ds(off, D)], bank[MSG0 + u % MSGN][:, 0:D],
                                ALU.add).then_inc(s_acc, 1)

            def message_group(layer, i, last, sort):
                for u in range(U):
                    t = i * U + u
                    n = i * U + (u + layer * T)
                    if sort:
                        sort_tile(1, t, u, n + (EC + 1))
                    if u < U - AHEAD or not last:
                        one_hot(layer, i * U + (u + AHEAD), (u + AHEAD) % U).then_inc(s_ohm, 1)
                    accumulate(layer, t, u, n)

            with dve.Fori(0, CI) as i:
                message_group(0, i, False, True)
            message_group(0, TI - 1, True, False)
            dve.wait_ge(s_acc, T + 1)

            with dve.Fori(0, NB) as b:
                V.bn_stats(bn6[:, ds(b, 1), :], x1_sb[:, ds(b, 1), :]).then_inc(s_agg[0], 1)
            dve.wait_ge(s_agg[0], NB)
            step(V.tensor_tensor(st_mean[:, :], bn6[:, :, 1], bn6[:, :, 4], ALU.add))
            step(V.tensor_tensor(st_sum[:, :], bn6[:, :, 1], bn6[:, :, 4], ALU.subtract))
            step(V.tensor_tensor(st_sum[:, :], st_sum[:, :], st_sum[:, :], ALU.mult))
            step(V.tensor_tensor(st_sq[:, :], bn6[:, :, 2], bn6[:, :, 5], ALU.add))
            step(V.scalar_tensor_tensor(st_sq[:, :], st_sum[:, :], D / 4.0, st_sq[:, :], ALU.mult, ALU.add))
            V.sem_inc(s_stats[1], 1)
            dve.wait_ge(s_std[1], 1)
            step(V.reciprocal(rstd[:, :], st_std[:, :]))
            step(V.scalar_tensor_tensor(shift[:, :], st_mean[:, :], -0.5, rstd[:, :], ALU.mult, ALU.mult))
            V.sem_inc(s_norm[1], 1)

            def stage_group(i, first):
                for u in range(TU):
                    if not first:
                        dve.wait_ge(s_stored[1][u], i * 16)
                    for g in range(G1):
                        dve.wait_ge(s_mm[1], i * (TU * G1) + (u * G1 + g + 1))
                        last = V.tensor_copy(stage1[:, u, 2 * g:2 * g + 2, :].rearrange("p r d -> p (r d)"),
                                             table_bank(g)[:, :])
                        last.then_inc(s_bankfree[1], 1)

            decode(1, 0)
            V.tensor_copy(agg1[:, :, :],
                          bias1[:, :].rearrange("p (b d) -> p b d", b=1).broadcast_to([P, NB, D]))
            stage_group(0, True)
            with dve.Fori(1, NB // TU) as i:
                stage_group(i, False)

            for t in range(AHEAD):
                V.tensor_scalar(oh_m[:, t, :], iota_p[:, :], local[:, t:t + 1], None,
                                ALU.is_equal).then_inc(s_ohm, 1)
            with dve.Fori(0, TI - 1) as i:
                message_group(1, i, False, False)
            message_group(1, TI - 1, True, False)
            dve.wait_ge(s_acc, 2 * T + 1)
            V.scalar_tensor_tensor(x1_sb[:, :, :], agg1[:, :, :], 0.0, x1_sb[:, :, :],
                                   ALU.max, ALU.add).then_inc(s_final, 1)

        @block.tensor
        def _(pe):
            TE = nc.tensor
            pe.sem_inc(s_sortfree, SR)

            def rank_products(layer):
                if layer == 0:
                    pe.wait_ge(s_const, 1)
                    pe.wait_ge(s_ident, 1)
                pe.wait_ge(s_rowtot[layer], 1)
                kw = dict(start=True, stop=True)
                TE.matmul(RANK[:, 0:NB], ones[0:EP, :], row_tot[:, :], **kw)
                TE.matmul(RANK[:, 32:32 + NB], before[0:EP, :], row_tot[:, :], **kw)
                TE.matmul(RANK[0:NB, 64:65], row_tot[:, :], ones[0:EP, 0:1], **kw).then_inc(s_total[layer], 1)
                pe.wait_ge(s_colend[layer], 1)
                TE.matmul(RANK[0:NB, 65:66], upto[0:NB, 0:NB], col_f[:, :], **kw).then_inc(s_colcum[layer], 1)
                pe.wait_ge(s_ended[layer], 1)
                TE.matmul(RANK[0:1, 0:T], ones[0:NB, 0:1], ended[:, :], **kw).then_inc(s_tilerow[layer], 1)

            def transposes(layer, i, u, first):
                n1 = i * TU + (u + 1)
                pe.wait_ge(s_h[layer], n1)
                if not first:
                    pe.wait_ge(s_hT[layer], i * TU + (u + 1 - TU))
                for k in range(KC):
                    last = TE.transpose(transposed(u)[:, k, :], h_ring[:, u, k * P:(k + 1) * P], ident[:, :])
                last.then_inc(s_tp[layer], 1)

            def table_rows(layer, i, u, first):
                n = i * TU + u
                pe.wait_ge(s_hT[layer], i * TU + (u + 1))
                for g in range(1 if layer == 0 else G1):
                    if layer == 0:
                        bk, w = table_bank(u)[:, 0:D], lambda k: w0_sb[:, k, :]
                        back = (1, 3, 2, 2, 2)[u]
                        if not (first and u < 2):
                            pe.wait_ge(s_staged[0], i * TU + (u + 1 - back))
                    else:
                        bk = table_bank(g)[:, :]
                        w = lambda k, g=g: w1_sb[:, k, 2 * g:2 * g + 2, :].rearrange("p r d -> p (r d)")
                        if not (first and u == 0 and g < 2):
                            pe.wait_ge(s_bankfree[1], i * (TU * G1) + (u * G1 + g + 1 - 2))
                    for k in range(KC):
                        last = TE.matmul(bk, hT_ring[:, u, k, :], w(k), start=(k == 0), stop=(k == KC - 1))
                    last.then_inc(s_mm[layer], 1)

            def table(layer):
                pe.wait_ge(s_w, 16 if layer == 0 else 16 * (1 + KC))
                if layer == 1:
                    pe.wait_ge(s_decoded[1], 1)
                for u in range(TU):
                    transposes(layer, 0, u, True)
                for u in range(TU):
                    table_rows(layer, 0, u, True)
                    transposes(layer, 1, u, False)
                with pe.Fori(1, NB // TU - 1) as i:
                    for u in range(TU):
                        table_rows(layer, i, u, False)
                        transposes(layer, i + 1, u, False)
                for u in range(TU):
                    table_rows(layer, NB // TU - 1, u, False)

            def sort_edges(layer, kind):
                for k in range(NSF[layer]):
                    last = TE.matmul(bank[k][:, 0:T], zeros16[0:EP, 0:P], zeros16[0:EP, :],
                                     start=(kind == "open"), stop=(kind == "close"))
                if kind == "close":
                    last.then_inc(s_sorted[layer], 1)

            def sort_tile(layer, u, n1):
                pe.wait_ge(s_sortready, n1)
                for k in range(NSF[layer]):
                    last = TE.matmul(bank[k][:, 0:T], oh_f[k][:, u % SR, :], oh_t[:, u % SR, :],
                                     start=False, stop=False)
                last.then_inc(s_sortfree, 1)

            def message(layer, i, u, first):
                n1 = i * U + (u + 1 + layer * T)
                pe.wait_ge(s_ohm, n1)
                pe.wait_ge(s_gather[u], i * 16 + 16 * (1 + layer * TI))
                if not (first and u < MSGN and layer == 0):
                    pe.wait_ge(s_acc, i * U + (u + 2 - MSGN + layer * T))
                TE.matmul(bank[MSG0 + u % MSGN][:, 0:D], oh_m[:, u, :], rows[:, u, :],
                          start=True, stop=True).then_inc(s_msg, 1)

            rank_products(0)
            table(0)
            pe.wait_ge(s_staged[0], NB)
            sort_edges(0, "open")
            with pe.Fori(0, CI) as i:
                for u in range(U):
                    sort_tile(0, u, i * U + (u + 1))
            sort_edges(0, "close")
            rank_products(1)
            pe.wait_ge(s_decoded[0], 1)
            sort_edges(1, "open")

            def group(layer, i, first, sort):
                for u in range(U):
                    message(layer, i, u, first)
                    if sort:
                        sort_tile(1, u, i * U + (EC + u + 1))

            group(0, 0, True, True)
            with pe.Fori(1, CI) as i:
                group(0, i, False, True)
            sort_edges(1, "close")
            group(0, TI - 1, False, False)
            table(1)
            group(1, 0, True, False)
            with pe.Fori(1, TI) as i:
                group(1, i, False, False)


_INS = ['x', 'src', 'dst', 'edge_type_8', 'edge_weight', 'L0_gnn_weight', 'L0_gnn_bias', 'L1_gnn_weight', 'L1_gnn_bias']
_OUTS = [((3125, 256), 'float32')]


def kernel(**inputs):
    import numpy as _np
    import concourse.bacc as _bacc
    from concourse import mybir as _mybir
    from concourse.bass_utils import run_bass_kernel_spmd as _run

    nc = _bacc.Bacc("TRN2", target_bir_lowering=False, num_devices=1)
    arrays, args = {}, []
    for name in _INS:
        a = _np.ascontiguousarray(inputs[name])
        arrays[f"in_{name}_dram"] = a
        args.append(nc.dram_tensor(f"in_{name}_dram", a.shape, _mybir.dt.from_np(a.dtype), kind="ExternalInput").ap())
    for i, (shape, dtype) in enumerate(_OUTS):
        dt = _mybir.dt.from_np(_np.dtype(dtype))
        args.append(nc.dram_tensor(f"out_{i}_dram", shape, dt, kind="ExternalOutput").ap())
    gnn_kernel(nc, *args)
    r = _run(nc, [arrays], core_ids=[0])
    return r.results[0]["out_0_dram"]
```

```python
import concourse.bass as bass
from concourse import mybir
from contextlib import ExitStack


def gnn_kernel(nc, x, src, dst, etype, ew, w0, b0, w1, b1, out):
    f32, i32 = mybir.dt.float32, mybir.dt.int32
    bf16, f16 = mybir.dt.bfloat16, mybir.dt.float16
    ALU = mybir.AluOpType
    ACT = mybir.ActivationFunctionType
    AX = mybir.AxisListType
    ds = bass.ds

    P = 128
    N, D = x.shape
    E = src.shape[0]
    R = w1.shape[0]
    KC = D // P
    NB = -(-N // P)
    NFULL = N // P
    NREST = N - NFULL * P
    NP = NB * P
    EP = 125
    EC = E // EP
    T = -(-E // P) + NB
    U = 16
    AHEAD = 8
    TI = T // U
    CI = EC // U
    assert EP * EC == E and TI * U == T and CI * U == EC and CI == NB and TI == CI + 1
    TU = 5
    assert NB % TU == 0 and D == KC * P and P == 128
    SR = 8
    G = 4
    EC0 = EC // 2
    U0 = EC0 // NB
    HALF = NB // 2 + 1
    assert U0 * NB == EC0 and U0 == 2 * G
    LAG = 4
    FR = 2
    RF = 4
    NSF = (5, 2)
    EPS = 1e-5
    KEY_LOW = 16

    table0 = nc.dram_tensor("table0", [NP, D], f32, kind="Internal").ap()
    table1 = nc.dram_tensor("table1", [R * NP, D], f32, kind="Internal").ap()
    tables = (table0, table1)
    scattered = nc.dram_tensor("scattered", [P * T, 2], f32, kind="Internal").ap()

    ctx = ExitStack()
    with ctx:
        def sb(name, shape, dt=f32):
            return ctx.enter_context(nc.sbuf_tensor(name, shape, dt))

        def sem(name):
            return ctx.enter_context(nc.semaphore(name))

        iota_p = sb("iota_p", [P, P])
        iota_g16 = sb("iota_g16", [P, P, G], f16)
        iota_t16 = sb("iota_t16", [P, T], f16)
        part = sb("part", [P, 1])
        ident = sb("ident", [P, P])
        before = sb("before", [P, P])
        upto = sb("upto", [NB, NB])
        ones = sb("ones", [P, P])
        zeros16 = sb("zeros16", [P, T], bf16)
        bias0 = sb("bias0", [P, D])
        bias1 = sb("bias1", [P, D])
        w0_sb = sb("w0_sb", [P, KC, D])
        x_sb = sb("x_sb", [P, NB, D])
        x1_sb = sb("x1_sb", [P, NB, D])
        agg1 = x_sb
        st_sum = sb("st_sum", [P, NB])
        st_sq = sb("st_sq", [P, NB])
        st_mean = sb("st_mean", [P, NB])
        st_std = sb("st_std", [P, NB])
        rstd = sb("rstd", [P, NB])
        shift = sb("shift", [P, NB])
        bn6 = sb("bn6", [P, NB, 6])
        eps_t = sb("eps_t", [P, 1])
        h_ring = sb("h_ring", [P, TU, D])
        hT_ring = sb("hT_ring", [P, TU, KC, P])
        src_i = sb("src_i", [EP, EC], i32)
        dst_i = sb("dst_i", [EP, EC], i32)
        type_i = sb("type_i", [EP, EC], i32)
        ew_f = sb("ew_f", [EP, EC])
        ew16 = [sb(f"ew16_{i}", [EP, EC], bf16) for i in range(3)]
        tmp_i = sb("tmp_i", [EP, EC], i32)
        tmp_f = sb("tmp_f", [EP, EC])
        row_f = sb("row_f", [EP, EC])
        bucket = sb("bucket", [EP, EC], f16)
        key_lo = sb("key_lo", [EP, EC])
        hi16 = [sb(f"hi16_{i}", [EP, EC], f16) for i in range(2)]
        lo16 = [sb(f"lo16_{i}", [EP, EC], f16) for i in range(2)]
        pos_t = [sb(f"pos_t{i}", [EP, EC]) for i in range(2)]
        pos_p = [sb(f"pos_p{i}", [EP, EC], f16) for i in range(2)]
        mask_mem = sb("mask_mem", [P, NB * EC], bf16)
        mask = mask_mem[0:EP, :].rearrange("p (b c) -> p b c", b=NB)
        w1_sb = mask_mem[:, 0:2 * KC * R * D].bitcast(f32).rearrange("p (k r d) -> p k r d", k=KC, r=R)
        scan = sb("scan", [P, P * 80])
        scan3 = scan[0:EP, 0:NB * EC].rearrange("p (b c) -> p b c", b=NB)
        stage1 = scan[:, 0:TU * R * D].rearrange("p (u r d) -> p u r d", u=TU, r=R)
        row_tot = sb("row_tot", [EP, NB])
        tot_i = sb("tot_i", [P, NB], i32)
        tiles_f = sb("tiles_f", [P, NB])
        tile_end = sb("tile_end", [P, NB])
        offs = sb("offs", [P, NB])
        col_i = sb("col_i", [NB, 1], i32)
        col_f = sb("col_f", [NB, 1])
        col_end = sb("col_end", [NB, 1])
        ended = h_ring[0:NB, 1:TU, :].rearrange("p u d -> p (u d)")[:, 0:T]
        tile_off = [sb(f"tile_off{i}", [1, T], i32) for i in range(2)]
        oh_t = sb("oh_t", [EP, SR, T], bf16)
        oh_p = sb("oh_p", [EP, FR, P, G], f16)
        idx = [sb(f"idx{i}", [P, T], i32) for i in range(2)]
        local = [sb(f"local{i}", [P, T]) for i in range(2)]
        ew_s = sb("ew_s", [P, T])
        idx_ring = sb("idx_ring", [P, U], i32)
        rows = sb("rows", [P, U, D])
        oh_f = [sb(f"oh_f{k}", [EP, FR, P, G], f16)[:, :, :, :] for k in range(2)] + [
            rows[0:EP, 2 * k:2 * k + 2, :].bitcast(bf16).rearrange("p (r u) d -> p r (u d)", r=FR)
            .rearrange("p r (m g) -> p r m g", g=G) for k in range(3)]
        back = rows[:, 8:12, :].rearrange("p u d -> p (u d)")[:, 0:2 * T].rearrange("p (t k) -> p t k", k=2)
        spare = hT_ring[0:EP, 1:TU, :, :].rearrange("p u k m -> p (u k m)")
        pay = spare[:, 0:2 * EC0].rearrange("p (c k) -> p c k", k=2)
        place = spare[:, 2 * EC0:3 * EC0].bitcast(i32)
        pay_ring = sb("pay_ring", [EP, U0, 2])
        place_ring = sb("place_ring", [EP, U0], i32)
        oh_m = sb("oh_m", [P, U, P])
        free0 = oh_m[:, :, :].rearrange("p u m -> p (u m)")
        scratch = (free0, scan)

        bank = [ctx.enter_context(nc.psum_tensor(f"bank{i}", [P, 512], f32)) for i in range(8)]

        def transposed(u):
            return bank[(0, 1, 2, 5, 6)[u]][:, 0:D].rearrange("p (k n) -> p k n", k=KC)

        def table_bank(g):
            return bank[3 + g % 2]
        RANK = bank[7]

        def message_bank(u):
            return bank[2 + u // 2 % 4][:, u % 2 * D:(u % 2 + 1) * D]
        RING = 8
        G1 = R // 2
        assert G1 == 4

        s_const = sem("s_const")
        s_ident = sem("s_ident")
        s_edges = sem("s_edges")
        s_x = sem("s_x")
        s_w = sem("s_w")
        s_bias = sem("s_bias")
        s_dve = sem("s_dve")
        s_act = sem("s_act")
        s_mask = sem("s_mask")
        s_scan = sem("s_scan")
        s_rowtot = [sem(f"s_rowtot{i}") for i in range(2)]
        s_total = [sem(f"s_total{i}") for i in range(2)]
        s_colend = [sem(f"s_colend{i}") for i in range(2)]
        s_colcum = [sem(f"s_colcum{i}") for i in range(2)]
        s_ended = [sem(f"s_ended{i}") for i in range(2)]
        s_tilerow = [sem(f"s_tilerow{i}") for i in range(2)]
        s_ohp = sem("s_ohp")
        s_sortready = sem("s_sortready")
        s_sortfree = sem("s_sortfree")
        s_sorted = [sem(f"s_sorted{i}") for i in range(2)]
        s_decoded = [sem(f"s_decoded{i}") for i in range(2)]
        s_stats = [sem(f"s_stats{i}") for i in range(2)]
        s_std = [sem(f"s_std{i}") for i in range(2)]
        s_norm = [sem(f"s_norm{i}") for i in range(2)]
        s_h = [sem(f"s_h{i}") for i in range(2)]
        s_tp = [sem(f"s_tp{i}") for i in range(2)]
        s_hT = [sem(f"s_hT{i}") for i in range(2)]
        s_mm = [sem(f"s_mm{i}") for i in range(2)]
        s_staged = [sem(f"s_staged{i}") for i in range(2)]
        s_stored0 = sem("s_stored0")
        s_stored1 = [sem(f"s_stored1_{u}") for u in range(TU)]
        s_bankfree = [sem(f"s_bankfree{i}") for i in range(2)]
        s_agg = [sem(f"s_agg{i}") for i in range(2)]
        s_idx = sem("s_idx")
        s_gather = [sem(f"s_gather{u}") for u in range(U)]
        s_ohm = sem("s_ohm")
        s_ohw = sem("s_ohw")
        s_msg = sem("s_msg")
        s_acc = sem("s_acc")
        s_final = sem("s_final")
        s_out = sem("s_out")
        s_place = sem("s_place")
        s_zero = sem("s_zero")
        s_zeroed = sem("s_zeroed")
        s_pay = sem("s_pay")
        s_payring = sem("s_payring")
        s_scat = [sem(f"s_scat{u}") for u in range(U0)]
        s_back = sem("s_back")

        block = ctx.enter_context(nc.Block())

        @block.sync
        def _(sp):
            def edges(a):
                return a.rearrange("(p c) -> p c", p=EP)
            sp.dma_start(dst_i[:, :], edges(dst)).then_inc(s_edges, 16)
            sp.dma_start(src_i[:, :], edges(src)).then_inc(s_edges, 16)
            sp.dma_start(type_i[:, :], edges(etype)).then_inc(s_edges, 16)
            sp.dma_start(ew_f[:, :], edges(ew)).then_inc(s_edges, 16)
            sp.wait_ge(s_zero, 1)
            sp.dma_start(scattered.rearrange("(p a t) k -> p a (t k)", p=P, a=4),
                         zeros16[:, :].bitcast(f32).rearrange("p (a t) -> p a t", a=1)
                         .broadcast_to([P, 4, T // 2])).then_inc(s_zeroed, 16)
            sp.wait_ge(s_const, 2)
            sp.dma_start(x_sb[0:NREST, NFULL, :], x[NFULL * P:N, :]).then_inc(s_x, 16)
            sp.dma_start(x_sb[:, 0:NFULL, :],
                         x[0:NFULL * P, :].rearrange("(b p) d -> p b d", p=P)).then_inc(s_x, 16)
            sp.dma_start(w0_sb[:, :, :], w0.rearrange("(k p) d -> p k d", p=P)).then_inc(s_w, 16)
            sp.dma_start(bias0[:, :], b0.partition_broadcast(P)).then_inc(s_bias, 16)
            sp.dma_start(bias1[:, :], b1.partition_broadcast(P)).then_inc(s_bias, 16)
            with sp.Fori(0, NB) as b:
                sp.wait_ge(s_staged[0], b + 1)
                sp.dma_start(table0[ds(b * P, P), :], x1_sb[:, ds(b, 1), :]).then_inc(s_stored0, 16)
            for u in range(U0):
                sp.wait_ge(s_scat[u], 16 * NB)
            sp.dma_start(back, scattered.rearrange("(p t) k -> p t k", p=P)).then_inc(s_back, 16)
            sp.wait_ge(s_place, 1)
            for k in range(KC):
                sp.dma_start(w1_sb[:, k, :, :],
                             w1[:, k * P:(k + 1) * P, :].rearrange("r p d -> p r d")).then_inc(s_w, 16)
            table1_rows = table1.rearrange("(r n) d -> n r d", r=R)
            with sp.Fori(0, NB // TU) as i:
                for u in range(TU):
                    sp.wait_ge(s_bankfree[1], i * (TU * G1) + (u + 1) * G1)
                    sp.dma_start(table1_rows[ds(i * (TU * P) + u * P, P), :, :],
                                 stage1[:, u, :, :]).then_inc(s_stored1[u], 16)
            sp.wait_ge(s_final, 1)
            sp.dma_start(out[0:NFULL * P, :].rearrange("(b p) d -> p b d", p=P),
                         x1_sb[:, 0:NFULL, :]).then_inc(s_out, 16)
            sp.dma_start(out[NFULL * P:N, :], x1_sb[0:NREST, NFULL, :]).then_inc(s_out, 16)
            sp.wait_ge(s_out, 32)

        @block.gpsimd
        def _(pool):
            allow = dict(allow_small_or_imprecise_dtypes=True)
            nc.gpsimd.iota(iota_p[:, :], pattern=[[1, P]], base=0, channel_multiplier=0, **allow)
            nc.gpsimd.iota(iota_g16[:, :, :], pattern=[[1, P], [0, G]], base=0, channel_multiplier=0, **allow)
            nc.gpsimd.iota(iota_t16[:, :], pattern=[[1, T]], base=0, channel_multiplier=0, **allow)
            nc.gpsimd.iota(part[:, :], pattern=[[0, 1]], base=0, channel_multiplier=1, **allow)
            nc.gpsimd.memset(zeros16[:, :], 0.0).then_inc(s_zero, 1)
            nc.gpsimd.memset(eps_t[:, :], EPS)
            nc.gpsimd.memset(ones[:, :], 1.0).then_inc(s_const, 1)
            nc.gpsimd.memset(x_sb[:, NFULL, :], 0.0).then_inc(s_const, 1)

            def scatter_columns(i, first):
                for u in range(U0):
                    if u % G == 0:
                        if not first:
                            for v in range(u, u + G):
                                pool.wait_ge(s_scat[v], i * 16)
                        nc.gpsimd.tensor_copy(pay_ring[:, u:u + G, :], pay[:, ds(i * U0 + u, G), :])
                        nc.gpsimd.tensor_copy(place_ring[:, u:u + G],
                                              place[:, ds(i * U0 + u, G)]).then_inc(s_payring, 1)
                        pool.wait_ge(s_payring, i * (U0 // G) + (u // G + 1))
                        pool.nop(nofuse=True)
                    pool.indirect_dma_start(
                        out=scattered[:, :],
                        out_offset=bass.IndirectOffsetOnAxis(ap=place_ring[:, u:u + 1], axis=0),
                        in_=pay_ring[:, u, :], in_offset=None).then_inc(s_scat[u], 16)

            pool.wait_ge(s_zeroed, 16)
            pool.wait_ge(s_pay, 1)
            scatter_columns(0, True)
            with pool.Fori(1, NB) as i:
                scatter_columns(i, False)
            for layer in range(2):
                if layer == 0:
                    pool.wait_ge(s_stored0, 16 * NB)
                else:
                    for u in range(TU):
                        pool.wait_ge(s_stored1[u], 16 * (NB // TU))
                with pool.Fori(0, TI) as i:
                    for u in range(U):
                        if u % RF == 0:
                            pool.wait_ge(s_idx, i * (U // RF) + (u // RF + layer * (T // RF) + 1))
                            pool.nop(nofuse=True)
                        pool.indirect_dma_start(
                            out=rows[:, u, :], out_offset=None, in_=tables[layer][:, :],
                            in_offset=bass.IndirectOffsetOnAxis(ap=idx_ring[:, u:u + 1], axis=0),
                        ).then_inc(s_gather[u], 16)

        @block.scalar
        def _(act):
            steps = [0]

            def step(ins):
                steps[0] += 1
                ins.then_inc(s_act, 1)
                act.wait_ge(s_act, steps[0])

            act.wait_ge(s_x, 32)
            act.wait_ge(s_const, 2)
            with act.Fori(0, NB) as b:
                nc.scalar.activation(x1_sb[:, ds(b, 1), :], x_sb[:, ds(b, 1), :], ACT.Identity, scale=-1.0 / D,
                                     accum_out=st_mean[:, ds(b, 1)]).then_inc(s_stats[0], 1)
            act.wait_ge(s_stats[0], NB)
            with act.Fori(0, NB) as b:
                nc.scalar.activation(x1_sb[:, ds(b, 1), :], x_sb[:, ds(b, 1), :], ACT.Square,
                                     bias=st_mean[:, ds(b, 1)],
                                     accum_out=st_sq[:, ds(b, 1)]).then_inc(s_stats[0], 1)
            act.wait_ge(s_stats[0], 2 * NB)
            nc.scalar.activation(st_std[:, :], st_sq[:, :], ACT.Sqrt, bias=eps_t[:, 0:1],
                                 scale=1.0 / D).then_inc(s_std[0], 1)

            act.wait_ge(s_norm[0], 1)
            with act.Fori(0, NB) as b:
                nc.scalar.activation(h_ring[:, 0, :], x_sb[:, ds(b, 1), :], ACT.Relu, bias=shift[:, ds(b, 1)],
                                     scale=rstd[:, ds(b, 1)]).then_inc(s_h[0], 1)
                act.wait_ge(s_tp[0], b + 1)
                nc.scalar.activation(hT_ring[:, 0, :, :], transposed(3), ACT.Copy).then_inc(s_hT[0], 1)
                act.wait_ge(s_mm[0], b + 1)
                nc.scalar.activation(x1_sb[:, ds(b, 1), :], bank[6][:, 0:D], ACT.Copy).then_inc(s_staged[0], 1)

            def refill(layer, u, t):
                nc.scalar.activation(idx_ring[:, u:u + RF], idx[layer][:, ds(t, RF)], ACT.Copy).then_inc(s_idx, 1)

            def feed(layer, i, last):
                for u in range(U):
                    if layer == 0 and not (last and u + AHEAD >= U):
                        if u % AHEAD == 0:
                            act.wait_ge(s_ohm, i * (U // AHEAD) + (u // AHEAD + 2))
                        scaled((u + AHEAD) % U, i * U + (u + AHEAD))
                    if u % RF == RF - 1 and not last:
                        act.wait_ge(s_msg, i * U + (u + 1 + layer * T))
                        refill(layer, u + 1 - RF, i * U + (u + 1 - RF + U))

            def scaled(u, t):
                nc.scalar.activation(oh_m[:, u, :], oh_m[:, u, :], ACT.Copy,
                                     scale=ew_s[:, ds(t, 1)]).then_inc(s_ohw, 1)

            for layer in range(2):
                if layer == 1:
                    act.wait_ge(s_stats[1], 1)
                    nc.scalar.activation(st_std[:, :], st_sq[:, :], ACT.Sqrt, bias=eps_t[:, 0:1],
                                         scale=1.0 / D).then_inc(s_std[1], 1)
                    act.wait_ge(s_norm[1], 1)
                    for u in range(TU):
                        nc.scalar.activation(h_ring[:, u, :], x1_sb[:, u, :], ACT.Relu, bias=shift[:, u:u + 1],
                                             scale=rstd[:, u:u + 1]).then_inc(s_h[1], 1)

                    def hidden_group(i, last):
                        for u in range(TU):
                            act.wait_ge(s_tp[1], i * TU + (u + 1))
                            if not isinstance(i, int) or i > 0:
                                act.wait_ge(s_mm[1], i * (TU * G1) + (u + 1 - TU) * G1)
                            nc.scalar.activation(hT_ring[:, u, :, :], transposed(u),
                                                 ACT.Copy).then_inc(s_hT[1], 1)
                            if not last:
                                b = i * TU + (u + TU)
                                nc.scalar.activation(h_ring[:, u, :], x1_sb[:, ds(b, 1), :], ACT.Relu,
                                                     bias=shift[:, ds(b, 1)],
                                                     scale=rstd[:, ds(b, 1)]).then_inc(s_h[1], 1)

                    hidden_group(0, False)
                    with act.Fori(1, NB // TU - 1) as i:
                        hidden_group(i, False)
                    hidden_group(NB // TU - 1, True)
                act.wait_ge(s_decoded[layer], 1)
                if layer == 1:
                    act.wait_ge(s_msg, T)
                for u in range(0, U, RF):
                    refill(layer, u, u)
                if layer == 0:
                    act.wait_ge(s_ohm, 1)
                    for u in range(AHEAD):
                        scaled(u, u)
                with act.Fori(0, TI - 1) as i:
                    feed(layer, i, False)
                feed(layer, TI - 1, True)

        @block.vector
        def _(dve):
            steps = [0]

            def step(ins):
                steps[0] += 1
                ins.then_inc(s_dve, 1)
                dve.wait_ge(s_dve, steps[0])

            V = nc.vector
            dve.sem_inc(s_acc, 1)
            dve.wait_ge(s_const, 1)
            V.tensor_scalar(before[:, :], iota_p[:, :], part[:, 0:1], None, ALU.is_gt)
            V.tensor_scalar(upto[:, :], iota_p[0:NB, 0:NB], part[0:NB, 0:1], None, ALU.is_ge)
            step(V.tensor_scalar(ident[:, :], iota_p[:, :], part[:, 0:1], None, ALU.is_equal))
            V.sem_inc(s_ident, 1)

            def keys(layer):
                key_hi = pos_t[layer]
                node, other = (dst_i, src_i) if layer == 0 else (src_i, dst_i)
                step(V.tensor_scalar(tmp_i[:, :], node[:, :], 7, None, ALU.logical_shift_right))
                step(V.tensor_copy(bucket[:, :], tmp_i[:, :]))
                step(V.tensor_scalar(tmp_i[:, :], node[:, :], P - 1, None, ALU.bitwise_and))
                step(V.tensor_copy(key_lo[:, :], tmp_i[:, :]))
                if layer == 0:
                    step(V.tensor_copy(row_f[:, :], other[:, :]))
                else:
                    step(V.tensor_copy(row_f[:, :], type_i[:, :]))
                    step(V.tensor_copy(tmp_f[:, :], other[:, :]))
                    step(V.scalar_tensor_tensor(row_f[:, :], row_f[:, :], float(NP), tmp_f[:, :],
                                                ALU.mult, ALU.add))
                step(V.tensor_copy(tmp_i[:, :], row_f[:, :]))
                step(V.tensor_scalar(tmp_i[:, :], tmp_i[:, :], 4, None, ALU.logical_shift_right))
                step(V.tensor_copy(key_hi[:, :], tmp_i[:, :]))
                step(V.scalar_tensor_tensor(tmp_f[:, :], key_hi[:, :], -float(KEY_LOW), row_f[:, :],
                                            ALU.mult, ALU.add))
                step(V.tensor_scalar(hi16[layer][:, :], key_hi[:, :], 1.0, None, ALU.add))
                step(V.scalar_tensor_tensor(lo16[layer][:, :], tmp_f[:, :], float(P), key_lo[:, :],
                                            ALU.mult, ALU.add))

            def masks(b):
                return V.tensor_scalar(mask[:, ds(b, 1), :], bucket[:, :], b_col(b), None, ALU.is_equal)

            def totals(layer):
                step(V.tensor_copy(row_tot[:, :], scan3[:, :, EC - 1]))
                V.sem_inc(s_rowtot[layer], 1)
                dve.wait_ge(s_total[layer], 1)
                step(V.tensor_scalar(tiles_f[:, :], RANK[:, 0:NB], float(P - 1), None, ALU.add))
                step(V.tensor_copy(tot_i[:, :], tiles_f[:, :]))
                step(V.tensor_scalar(tot_i[:, :], tot_i[:, :], 7, None, ALU.logical_shift_right))
                step(V.tensor_copy(tiles_f[:, :], tot_i[:, :]))
                step(V.tensor_tensor_scan(tile_end[:, :], tiles_f[:, :], tiles_f[:, :], 0.0,
                                          ALU.add, ALU.max))
                step(V.tensor_tensor(tile_end[:, :], tile_end[:, :], tiles_f[:, :], ALU.subtract))
                step(V.tensor_scalar(tile_end[:, :], tile_end[:, :], float(P), -1.0, ALU.mult, ALU.add))
                step(V.tensor_tensor(offs[0:EP, :], tile_end[0:EP, :], RANK[0:EP, 32:32 + NB], ALU.add))
                step(V.tensor_scalar(col_f[:, :], RANK[0:NB, 64:65], float(P - 1), None, ALU.add))
                step(V.tensor_copy(col_i[:, :], col_f[:, :]))
                step(V.tensor_scalar(col_i[:, :], col_i[:, :], 7, None, ALU.logical_shift_right))
                V.tensor_copy(col_f[:, :], col_i[:, :]).then_inc(s_colend[layer], 1)
                dve.wait_ge(s_colcum[layer], 1)
                step(V.tensor_copy(col_end[:, :], RANK[0:NB, 65:66]))
                V.tensor_scalar(ended, iota_t16[0:NB, :], col_end[:, 0:1], None,
                                ALU.is_ge).then_inc(s_ended[layer], 1)
                dve.wait_ge(s_tilerow[layer], 1)
                step(V.tensor_scalar(tile_off[layer][:, :], RANK[0:1, 0:T], float(NB - 1), float(D),
                                     ALU.min, ALU.mult))

            def place_block(b):
                return V.scalar_tensor_tensor(scan3[:, ds(b, 1), :], scan3[:, ds(b, 1), :], offs[0:EP, ds(b, 1)],
                                              mask[:, ds(b, 1), :], ALU.add, ALU.mult)

            def positions(layer):
                step(V.tensor_reduce(tmp_f[:, :], scan3.rearrange("p b c -> p c b"), AX.X, ALU.add))
                step(V.tensor_copy(tmp_i[:, :], tmp_f[:, :]))
                step(V.tensor_scalar(tmp_i[:, :], tmp_i[:, :], 7, None, ALU.logical_shift_right))
                step(V.tensor_copy(pos_t[layer][:, :], tmp_i[:, :]))
                step(V.scalar_tensor_tensor(pos_p[layer][:, :], pos_t[layer][:, :], -float(P), tmp_f[:, :],
                                            ALU.mult, ALU.add))

            b_tab = iota_p

            def b_col(b):
                return b_tab[0:EP, ds(b, 1)]

            def scan_block(b):
                m = mask[:, ds(b, 1), :].rearrange("p a c -> p (a c)")
                s = scan3[:, ds(b, 1), :].rearrange("p a c -> p (a c)")
                return V.tensor_tensor_scan(s, m, m, 0.0, ALU.add, ALU.max)

            def sort_fields(layer, i, u):
                c = i * (U if layer else U0) + u
                r = u // G % FR
                dve.wait_ge(s_sortfree, c + (SR - G + layer * EC0))
                own = [EP, P, G]
                def cols(a):
                    return a[:, ds(c, G)].rearrange("p (m g) -> p m g", m=1).broadcast_to(own)
                V.tensor_tensor(oh_p[:, r, :, :], iota_g16[0:EP, :, :], cols(pos_p[layer]),
                                ALU.is_equal).then_inc(s_ohp, 1)
                dve.wait_ge(s_ohp, i * ((U if layer else U0) // G) + (u // G + 1 + layer * (EC0 // G)))
                for k, f in enumerate([hi16[layer], lo16[layer]] + (ew16 if layer == 0 else [])):
                    V.tensor_tensor(oh_f[k][:, r, :, :], oh_p[:, r, :, :], cols(f), ALU.mult)

            def sort_tile(layer, c, u):
                V.tensor_scalar(oh_t[:, u % SR, :], iota_t16[0:EP, :], pos_t[layer][:, ds(c, 1)], None,
                                ALU.is_equal).then_inc(s_sortready, 1)

            def decode(layer, bk):
                dve.wait_ge(s_sorted[layer], 1)
                dec_i, dec_j = (scratch[layer][:, k * T:(k + 1) * T].bitcast(i32) for k in (0, 1))
                dec_f, dec_g = (scratch[layer][:, k * T:(k + 1) * T] for k in (2, 3))
                step(V.tensor_copy(dec_g, bank[bk][:, 0:T]))
                step(V.scalar_tensor_tensor(dec_f, dec_g, float(KEY_LOW * P), bank[bk + 1][:, 0:T],
                                            ALU.mult, ALU.add))
                if layer == 0:
                    dve.wait_ge(s_back, 16)
                    step(V.tensor_tensor(dec_f, dec_f, back[:, :, 0], ALU.add))
                step(V.tensor_copy(dec_i, dec_f))
                step(V.tensor_scalar(dec_j, dec_i, 7, None, ALU.logical_shift_right))
                step(V.tensor_copy(dec_g, dec_j))
                step(V.tensor_scalar(idx[layer][:, :], dec_g, -float(KEY_LOW), 0.0, ALU.add, ALU.max))
                step(V.tensor_scalar(dec_j, dec_i, P - 1, None, ALU.bitwise_and))
                step(V.tensor_copy(local[layer][:, :], dec_j))
                step(V.tensor_scalar(dec_g, dec_f, 0.0, -2.0 * P, ALU.is_equal, ALU.mult))
                step(V.tensor_tensor(local[layer][:, :], local[layer][:, :], dec_g, ALU.add))
                if layer == 0:
                    step(V.tensor_copy(dec_g, bank[bk + 2][:, 0:T]))
                    step(V.tensor_tensor(dec_g, dec_g, bank[bk + 3][:, 0:T], ALU.add))
                    step(V.tensor_tensor(dec_g, dec_g, bank[bk + 4][:, 0:T], ALU.add))
                    step(V.tensor_tensor(ew_s[:, :], dec_g, back[:, :, 1], ALU.add))
                V.sem_inc(s_decoded[layer], 1)

            def one_hots(layer, t, u):
                own = [P, AHEAD, P]
                V.tensor_tensor(oh_m[:, u:u + AHEAD, :],
                                iota_p[:, :].rearrange("p (a m) -> p a m", a=1).broadcast_to(own),
                                local[layer][:, ds(t, AHEAD)].rearrange("p (a m) -> p a m", m=1).broadcast_to(own),
                                ALU.is_equal).then_inc(s_ohm, 1)

            dve.wait_ge(s_edges, 64)
            keys(0)
            step(V.tensor_copy(ew16[0][:, :], ew_f[:, :]))
            step(V.tensor_tensor(tmp_f[:, :], ew_f[:, :], ew16[0][:, :], ALU.subtract))
            step(V.tensor_copy(ew16[1][:, :], tmp_f[:, :]))
            step(V.tensor_tensor(ew16[2][:, :], tmp_f[:, :], ew16[1][:, :], ALU.subtract))
            with dve.Fori(0, NB) as b:
                masks(b).then_inc(s_mask, 1)
            dve.wait_ge(s_mask, NB)
            with dve.Fori(0, NB) as b:
                scan_block(b).then_inc(s_scan, 1)
            dve.wait_ge(s_scan, NB)
            totals(0)
            with dve.Fori(0, NB) as b:
                place_block(b).then_inc(s_scan, 1)
            dve.wait_ge(s_scan, 2 * NB)
            positions(0)

            own = slice(EC0, EC)
            step(V.scalar_tensor_tensor(pay[:, :, 0], hi16[0][:, own], float(KEY_LOW * P), lo16[0][:, own],
                                        ALU.mult, ALU.add))
            step(V.tensor_copy(pay[:, :, 1], ew_f[:, own]))
            step(V.scalar_tensor_tensor(place, pos_p[0][:, own], float(T), pos_t[0][:, own], ALU.mult, ALU.add))
            V.sem_inc(s_pay, 1)

            def sort_group(i):
                for u in range(U0):
                    if u % G == 0:
                        sort_fields(0, i, u)
                    sort_tile(0, i * U0 + u, u)

            def rank_block(b):
                masks(b).then_inc(s_mask, 1)
                dve.wait_ge(s_mask, b + (NB + 1))
                scan_block(b).then_inc(s_scan, 1)

            dve.wait_ge(s_std[0], 1)
            step(V.reciprocal(rstd[:, :], st_std[:, :]))
            step(V.tensor_tensor(shift[:, :], st_mean[:, :], rstd[:, :], ALU.mult))
            V.sem_inc(s_norm[0], 1)
            sort_group(0)
            keys(1)
            rank_block(0)
            with dve.Fori(1, HALF) as i:
                sort_group(i)
                rank_block(i * 2 - 1)
                rank_block(i * 2)
            dve.wait_ge(s_scan, 3 * NB)
            totals(1)
            with dve.Fori(HALF, NB) as i:
                sort_group(i)
                for k in range(2):
                    place_block(i * 2 + (k - 2 * HALF)).then_inc(s_scan, 1)
            place_block(NB - 1).then_inc(s_scan, 1)
            dve.wait_ge(s_scan, 4 * NB)
            V.sem_inc(s_place, 1)
            positions(1)
            dve.wait_ge(s_bias, 32)
            dve.wait_ge(s_stored0, 16 * NB)
            V.tensor_tensor(x1_sb[:, :, :], x_sb[:, :, :],
                            bias0[:, :].rearrange("p (b d) -> p b d", b=1).broadcast_to([P, NB, D]), ALU.add)
            decode(0, 0)
            one_hots(0, 0, 0)

            def offsets(layer, t):
                _, offs = nc.values_load_multi_w_load_instructions(
                    tile_off[layer][0:1, ds(t, LAG)], engines=[mybir.EngineType.DVE], min_val=0,
                    max_val=(NB - 1) * D, skip_runtime_bounds_check_because="totals() clamps them")
                return offs

            def accumulate(layer, off, u, n):
                acc = (x1_sb if layer == 0 else agg1)[:, :, :].rearrange("p b d -> p (b d)")
                dve.wait_ge(s_acc, n + 1)
                V.tensor_tensor(acc[:, ds(off, D)], acc[:, ds(off, D)], message_bank(u), ALU.add).then_inc(s_acc, 1)

            def message_group(layer, i, first, last, sort):
                for u in range(U):
                    if u % LAG == 0 and (u >= LAG or not first):
                        offs = offsets(layer, i * U + (u - LAG))
                    if sort and u % G == 0:
                        sort_fields(1, i, u)
                    if u % 2 == 0 and (u >= LAG or not first):
                        dve.wait_ge(s_msg, i * U + (u - LAG + layer * T + 2))
                    if sort:
                        sort_tile(1, i * U + u, u)
                    if u % AHEAD == LAG and not (last and u + AHEAD > U):
                        one_hots(layer, i * U + (u + AHEAD - LAG), (u + AHEAD - LAG) % U)
                    if u >= LAG or not first:
                        accumulate(layer, offs[u % LAG], (u - LAG) % U, i * U + (u - LAG + layer * T))
                if last:
                    dve.wait_ge(s_msg, i * U + (U + layer * T))
                    offs = offsets(layer, i * U + (U - LAG))
                    for u in range(U - LAG, U):
                        accumulate(layer, offs[u % LAG], u, i * U + (u + layer * T))

            message_group(0, 0, True, False, True)
            with dve.Fori(1, CI) as i:
                message_group(0, i, False, False, True)
            decode(1, 0)
            message_group(0, TI - 1, False, True, False)
            dve.wait_ge(s_acc, T + 1)

            with dve.Fori(0, NB) as b:
                V.bn_stats(bn6[:, ds(b, 1), :], x1_sb[:, ds(b, 1), :]).then_inc(s_agg[0], 1)
            dve.wait_ge(s_agg[0], NB)
            step(V.tensor_tensor(st_mean[:, :], bn6[:, :, 1], bn6[:, :, 4], ALU.add))
            step(V.tensor_tensor(st_sum[:, :], bn6[:, :, 1], bn6[:, :, 4], ALU.subtract))
            step(V.tensor_tensor(st_sum[:, :], st_sum[:, :], st_sum[:, :], ALU.mult))
            step(V.tensor_tensor(st_sq[:, :], bn6[:, :, 2], bn6[:, :, 5], ALU.add))
            step(V.scalar_tensor_tensor(st_sq[:, :], st_sum[:, :], D / 4.0, st_sq[:, :], ALU.mult, ALU.add))
            V.sem_inc(s_stats[1], 1)
            dve.wait_ge(s_std[1], 1)
            step(V.reciprocal(rstd[:, :], st_std[:, :]))
            step(V.scalar_tensor_tensor(shift[:, :], st_mean[:, :], -0.5, rstd[:, :], ALU.mult, ALU.mult))
            V.sem_inc(s_norm[1], 1)

            def stage_group(i, first):
                for u in range(TU):
                    if not first:
                        dve.wait_ge(s_stored1[u], i * 16)
                    for g in range(G1):
                        dve.wait_ge(s_mm[1], i * (TU * G1) + (u * G1 + g + 1))
                        last = V.tensor_copy(stage1[:, u, 2 * g:2 * g + 2, :].rearrange("p r d -> p (r d)"),
                                             table_bank(g)[:, :])
                        last.then_inc(s_bankfree[1], 1)

            V.tensor_copy(agg1[:, :, :],
                          bias1[:, :].rearrange("p (b d) -> p b d", b=1).broadcast_to([P, NB, D]))
            stage_group(0, True)
            with dve.Fori(1, NB // TU) as i:
                stage_group(i, False)

            one_hots(1, 0, 0)
            message_group(1, 0, True, False, False)
            with dve.Fori(1, TI - 1) as i:
                message_group(1, i, False, False, False)
            message_group(1, TI - 1, False, True, False)
            dve.wait_ge(s_acc, 2 * T + 1)
            V.scalar_tensor_tensor(x1_sb[:, :, :], agg1[:, :, :], 0.0, x1_sb[:, :, :],
                                   ALU.max, ALU.add).then_inc(s_final, 1)

        @block.tensor
        def _(pe):
            TE = nc.tensor
            pe.sem_inc(s_sortfree, SR)

            def rank_products(layer):
                if layer == 0:
                    pe.wait_ge(s_const, 1)
                    pe.wait_ge(s_ident, 1)
                pe.wait_ge(s_rowtot[layer], 1)
                kw = dict(start=True, stop=True)
                TE.matmul(RANK[:, 0:NB], ones[0:EP, :], row_tot[:, :], **kw)
                TE.matmul(RANK[:, 32:32 + NB], before[0:EP, :], row_tot[:, :], **kw)
                TE.matmul(RANK[0:NB, 64:65], row_tot[:, :], ones[0:EP, 0:1], **kw).then_inc(s_total[layer], 1)
                pe.wait_ge(s_colend[layer], 1)
                TE.matmul(RANK[0:NB, 65:66], upto[:, :], col_f[:, :], **kw).then_inc(s_colcum[layer], 1)
                pe.wait_ge(s_ended[layer], 1)
                TE.matmul(RANK[0:1, 0:T], ones[0:NB, 0:1], ended, **kw).then_inc(s_tilerow[layer], 1)

            def transposes(i, u, first):
                pe.wait_ge(s_h[1], i * TU + (u + 1))
                if not first:
                    pe.wait_ge(s_hT[1], i * TU + (u + 1 - TU))
                for k in range(KC):
                    last = TE.transpose(transposed(u)[:, k, :], h_ring[:, u, k * P:(k + 1) * P], ident[:, :])
                last.then_inc(s_tp[1], 1)

            def table_rows(i, u, first):
                pe.wait_ge(s_hT[1], i * TU + (u + 1))
                for g in range(G1):
                    if not (first and u == 0 and g < 2):
                        pe.wait_ge(s_bankfree[1], i * (TU * G1) + (u * G1 + g + 1 - 2))
                    for k in range(KC):
                        last = TE.matmul(table_bank(g)[:, :], hT_ring[:, u, k, :],
                                         w1_sb[:, k, 2 * g:2 * g + 2, :].rearrange("p r d -> p (r d)"),
                                         start=(k == 0), stop=(k == KC - 1))
                    last.then_inc(s_mm[1], 1)

            def table():
                pe.wait_ge(s_w, 16 * (1 + KC))
                for u in range(TU):
                    transposes(0, u, True)
                for u in range(TU):
                    table_rows(0, u, True)
                    transposes(1, u, False)
                with pe.Fori(1, NB // TU - 1) as i:
                    for u in range(TU):
                        table_rows(i, u, False)
                        transposes(i + 1, u, False)
                for u in range(TU):
                    table_rows(NB // TU - 1, u, False)

            def sort_edges(layer, kind):
                for k in range(NSF[layer]):
                    last = TE.matmul(bank[k][:, 0:T], zeros16[0:EP, 0:P], zeros16[0:EP, :],
                                     start=(kind == "open"), stop=(kind == "close"))
                if kind == "close":
                    last.then_inc(s_sorted[layer], 1)

            def sort_tile(layer, u, n1):
                pe.wait_ge(s_sortready, n1)
                for k in range(NSF[layer]):
                    last = TE.matmul(bank[k][:, 0:T], oh_f[k][:, u // G % FR, :, u % G], oh_t[:, u % SR, :],
                                     start=False, stop=False)
                last.then_inc(s_sortfree, 1)

            def message(layer, i, u, first):
                n1 = i * U + (u + 1 + layer * T)
                if layer == 0:
                    pe.wait_ge(s_ohw, n1)
                else:
                    pe.wait_ge(s_ohm, i * (U // AHEAD) + (u // AHEAD + 1 + T // AHEAD))
                pe.wait_ge(s_gather[u], i * 16 + 16 * (1 + layer * TI))
                if u % 2 == 0 and not (first and u < RING and layer == 0):
                    pe.wait_ge(s_acc, i * U + (u + 3 - RING + layer * T))
                TE.matmul(message_bank(u), oh_m[:, u, :], rows[:, u, :],
                          start=True, stop=True).then_inc(s_msg, 1)

            rank_products(0)
            pe.wait_ge(s_w, 16)
            sort_edges(0, "open")
            def sort_group(i):
                for u in range(U0):
                    sort_tile(0, u, i * U0 + (u + 1))
                    if u == 1:
                        pe.wait_ge(s_h[0], i + 1)
                        for k in range(KC):
                            last = TE.transpose(transposed(3)[:, k, :], h_ring[:, 0, k * P:(k + 1) * P],
                                                ident[:, :])
                        last.then_inc(s_tp[0], 1)
                    if u == 5:
                        pe.wait_ge(s_hT[0], i + 1)
                        for k in range(KC):
                            last = TE.matmul(bank[6][:, 0:D], hT_ring[:, 0, k, :], w0_sb[:, k, :],
                                             start=(k == 0), stop=(k == KC - 1))
                        last.then_inc(s_mm[0], 1)

            with pe.Fori(0, HALF) as i:
                sort_group(i)
            rank_products(1)
            with pe.Fori(HALF, NB) as i:
                sort_group(i)
            sort_edges(0, "close")
            pe.wait_ge(s_decoded[0], 1)
            sort_edges(1, "open")

            def group(layer, i, first, sort):
                for u in range(U):
                    message(layer, i, u, first)
                    if sort:
                        sort_tile(1, u, i * U + (EC0 + u + 1))

            group(0, 0, True, True)
            with pe.Fori(1, CI) as i:
                group(0, i, False, True)
            sort_edges(1, "close")
            group(0, TI - 1, False, False)
            table()
            group(1, 0, True, False)
            with pe.Fori(1, TI) as i:
                group(1, i, False, False)


_INS = ['x', 'src', 'dst', 'edge_type_8', 'edge_weight', 'L0_gnn_weight', 'L0_gnn_bias', 'L1_gnn_weight', 'L1_gnn_bias']
_OUTS = [((3125, 256), 'float32')]


def kernel(**inputs):
    import numpy as _np
    import concourse.bacc as _bacc
    from concourse import mybir as _mybir
    from concourse.bass_utils import run_bass_kernel_spmd as _run

    nc = _bacc.Bacc("TRN2", target_bir_lowering=False, num_devices=1)
    arrays, args = {}, []
    for name in _INS:
        a = _np.ascontiguousarray(inputs[name])
        arrays[f"in_{name}_dram"] = a
        args.append(nc.dram_tensor(f"in_{name}_dram", a.shape, _mybir.dt.from_np(a.dtype), kind="ExternalInput").ap())
    for i, (shape, dtype) in enumerate(_OUTS):
        dt = _mybir.dt.from_np(_np.dtype(dtype))
        args.append(nc.dram_tensor(f"out_{i}_dram", shape, dt, kind="ExternalOutput").ap())
    gnn_kernel(nc, *args)
    r = _run(nc, [arrays], core_ids=[0])
    return r.results[0]["out_0_dram"]
```

```python
import concourse.bass as bass
from concourse import mybir
from contextlib import ExitStack


def gnn_kernel(nc, x, src, dst, etype, ew, w0, b0, w1, b1, out):
    f32, i32 = mybir.dt.float32, mybir.dt.int32
    bf16, f16, f32r = mybir.dt.bfloat16, mybir.dt.float16, mybir.dt.float32r
    ALU = mybir.AluOpType
    ACT = mybir.ActivationFunctionType
    ds = bass.ds

    P = 128
    N, D = x.shape
    E = src.shape[0]
    R = w1.shape[0]
    KC = D // P
    NB = -(-N // P)
    NFULL = N // P
    NREST = N - NFULL * P
    NP = NB * P
    EP = 125
    EC = E // EP
    T = -(-E // P) + NB
    U = 16
    AHEAD = 8
    TI = T // U
    assert EP * EC == E and TI * U == T
    DONE = [(E + (P - 1) * (b + 1)) // P + 1 for b in range(NB - 1)] + [T]
    TU = 5
    assert NB % TU == 0 and D == KC * P and P == 128
    SR = 8
    G = 4
    U0 = 2 * G
    STEPS0 = NB + 1
    EC0 = STEPS0 * U0
    SCAT0 = (EC - EC0) // U0
    EC1 = 20 * U
    HALF = NB // 2 + 1
    SORT1 = range(1, 1 + EC1 // U)
    SCAT1 = (EC - EC1) // U0
    assert (SCAT0 + STEPS0) * U0 == EC and SCAT1 * U0 + EC1 == EC
    LAG = 4
    FR = 2
    RF = 4
    NSF = (5, 2)
    EPS = 1e-5
    KEY_LOW = 16

    table0 = nc.dram_tensor("table0", [NP, D], f32, kind="Internal").ap()
    table1 = nc.dram_tensor("table1", [R * NP, D], f32, kind="Internal").ap()
    tables = (table0, table1)
    scattered = [nc.dram_tensor(f"scattered{i}", [P * T, 2 - i], f32, kind="Internal").ap() for i in range(2)]

    ctx = ExitStack()
    with ctx:
        def sb(name, shape, dt=f32):
            return ctx.enter_context(nc.sbuf_tensor(name, shape, dt))

        at = {}

        def sb_under(name, shape, dt=f32):
            at[name] = nc.sbuf_base
            return sb(name, shape, dt)

        def sb_over(under, name, shape, dt):
            return nc.alloc_sbuf_tensor_at(name, shape, dt, offset=at[under])

        def sem(name):
            return ctx.enter_context(nc.semaphore(name))

        iota_p = sb("iota_p", [P, P])
        iota_g16 = sb("iota_g16", [P, P, G], f16)
        iota_t16 = sb("iota_t16", [P, T], f16)
        part = sb("part", [P, 1])
        ident = sb("ident", [P, P])
        before = sb("before", [P, P])
        upto = sb("upto", [NB, NB])
        ones = sb("ones", [P, P])
        zeros16 = sb("zeros16", [P, T], bf16)
        bias0 = sb("bias0", [P, D])
        bias1 = sb("bias1", [P, D])
        w0_sb = sb("w0_sb", [P, KC, D])
        x_sb = sb("x_sb", [P, NB, D])
        x1_sb = sb("x1_sb", [P, NB, D])
        agg1 = x_sb
        st_sum = sb("st_sum", [P, NB])
        st_sq = sb("st_sq", [P, NB])
        st_mean = sb("st_mean", [P, NB])
        st_std = sb("st_std", [P, NB])
        rstd = sb("rstd", [P, NB])
        shift = sb("shift", [P, NB])
        bn6 = sb("bn6", [P, NB, 6])
        eps_t = sb("eps_t", [P, 1])
        h_ring = sb("h_ring", [P, TU, D])
        hT_ring = sb_under("hT_ring", [P, TU, KC, P])
        hT_hi = sb_over("hT_ring", "hT_hi", [P, TU, KC, P], f32r)
        edge_mem = sb_under("edge_mem", [P, KC * R * D])
        w1_hi = sb_over("edge_mem", "w1_hi", [P, KC, R, D], f32r)
        edge_mem = edge_mem[0:EP, 0:10 * EC].rearrange("p (a c) -> p a c", a=10)
        src_i, dst_i, type_i, tmp_i = (edge_mem[:, k, :].bitcast(i32) for k in range(4))
        ew_f, tmp_f, key_lo = (edge_mem[:, 4 + k, :] for k in range(3))
        pos_t = [edge_mem[:, 7 + k, :] for k in range(2)]
        ew16, ew16_0 = (sb(f"ew16_{i}", [EP, EC0], bf16) for i in range(2))
        ew_part = [sb(f"ew_part{i}", [EP, EC0]) for i in (1, 2)]
        row_f = sb("row_f", [EP, EC])
        bucket = sb("bucket", [EP, EC], f16)
        hi = [sb("hi16", [EP, EC], f16), edge_mem[:, 9, :]]
        lo = [sb("lo16", [EP, EC], f16), sb("lo1", [EP, EC])]
        pos_p = [sb(f"pos_p{i}", [EP, EC], f16) for i in range(2)]
        mask_mem = sb_under("mask_mem", [P, NB * EC], bf16)
        mask = mask_mem[0:EP, :].rearrange("p (b c) -> p b c", b=NB)
        w1_sb = mask_mem[:, 0:2 * KC * R * D].bitcast(f32).rearrange("p (k r d) -> p k r d", k=KC, r=R)
        w1_lo = sb_over("mask_mem", "w1_lo", [P, KC, R, D], f32r)
        scan = sb("scan", [P, P * 80])
        scan3 = scan[0:EP, 0:NB * EC].rearrange("p (b c) -> p b c", b=NB)
        stage1 = scan[:, 0:TU * R * D].rearrange("p (u r d) -> p u r d", u=TU, r=R)
        row_tot = sb("row_tot", [EP, NB])
        tot_i = sb("tot_i", [P, NB], i32)
        tiles_f = sb("tiles_f", [P, NB])
        tile_end = sb("tile_end", [P, NB])
        offs = sb("offs", [P, NB])
        col_i = sb("col_i", [NB, 1], i32)
        col_f = sb("col_f", [NB, 1])
        col_end = sb("col_end", [NB, 1])
        ended = h_ring[0:NB, 1:TU, :].rearrange("p u d -> p (u d)")[:, 0:T]
        tile_off = [sb(f"tile_off{i}", [1, T], i32) for i in range(2)]
        oh_t = sb_under("oh_t", [EP, SR, T], bf16)
        hT_lo = sb_over("oh_t", "hT_lo", [P, TU, KC, P], f32r)
        oh_p = sb("oh_p", [EP, FR, P, G], f16)
        idx = [sb(f"idx{i}", [P, T], i32) for i in range(2)]
        local = [sb(f"local{i}", [P, T]) for i in range(2)]
        ew_s = sb("ew_s", [P, T])
        idx_ring = sb("idx_ring", [P, U], i32)
        rows = sb("rows", [P, U, D])
        oh_f = [sb(f"oh_f{k}", [EP, FR, P, G], f16)[:, :, :, :] for k in range(2)] + [
            rows[0:EP, 2 * k:2 * k + 2, :].bitcast(bf16).rearrange("p (r u) d -> p r (u d)", r=FR)
            .rearrange("p r (m g) -> p r m g", g=G) for k in range(3)]
        back = rows[:, U - RF:U, :].rearrange("p u d -> p (u d)")[:, 0:2 * T].rearrange("p (t k) -> p t k", k=2)
        stage0 = rows[:, 6, :]
        back1 = rows[:, 0:2, :].rearrange("p u d -> p (u d)")[:, 0:T]
        pay1 = row_f[:, 0:EC - EC1]
        place1 = row_f[:, EC - EC1:2 * (EC - EC1)].bitcast(i32)
        key_hold = mask_mem[:, 2 * KC * R * D:2 * KC * R * D + 2 * T].bitcast(f32)
        spare = hT_ring[0:EP, 1:TU, :, :].rearrange("p u k m -> p (u k m)")
        pay = spare[:, 0:2 * (EC - EC0)].rearrange("p (c k) -> p c k", k=2)
        place = spare[:, 2 * (EC - EC0):3 * (EC - EC0)].bitcast(i32)
        pay_ring = sb("pay_ring", [EP, U0, 2])
        place_ring = sb("place_ring", [EP, U0], i32)
        oh_m = sb("oh_m", [P, U, P])
        free0 = oh_m[:, :, :].rearrange("p u m -> p (u m)")

        bank = [ctx.enter_context(nc.psum_tensor(f"bank{i}", [P, 512], f32)) for i in range(8)]

        TB = (0, 1, 6, 7)
        assert TU == len(TB) + 1

        def transposed(u):
            return bank[TB[u % len(TB)]][:, 0:D].rearrange("p (k n) -> p k n", k=KC)

        def table_bank(g):
            return bank[2 + g]
        bank_h0 = bank[5][:, 0:D].rearrange("p (k n) -> p k n", k=KC)
        RANK = bank[7]

        def column(layer, k):
            return (bank[6] if layer == 0 else RANK)[0:NB, 64 + k:65 + k]

        def message_bank(u):
            return bank[2 + u // 2 % 4][:, u % 2 * D:(u % 2 + 1) * D]
        RING = 8
        G1 = R // 2
        assert G1 == 4

        s_const = sem("s_const")
        s_ident = sem("s_ident")
        s_dst = sem("s_dst")
        s_edges = sem("s_edges")
        s_x = sem("s_x")
        s_w = sem("s_w")
        s_bias = sem("s_bias")
        s_dve = sem("s_dve")
        s_mask = sem("s_mask")
        s_scan = sem("s_scan")
        s_placed = sem("s_placed")
        s_possum = [sem(f"s_possum{i}") for i in range(2)]
        s_x1 = sem("s_x1")
        s_agginit = sem("s_agginit")
        s_rowtot = [sem(f"s_rowtot{i}") for i in range(2)]
        s_total = [sem(f"s_total{i}") for i in range(2)]
        s_colend = [sem(f"s_colend{i}") for i in range(2)]
        s_colcum = [sem(f"s_colcum{i}") for i in range(2)]
        s_ended = [sem(f"s_ended{i}") for i in range(2)]
        s_tilerow = [sem(f"s_tilerow{i}") for i in range(2)]
        s_ohp = sem("s_ohp")
        s_ewpart = sem("s_ewpart")
        s_sortready = sem("s_sortready")
        s_fieldready = sem("s_fieldready")
        s_sortfree = sem("s_sortfree")
        s_sorted = [sem(f"s_sorted{i}") for i in range(2)]
        s_index = [sem(f"s_index{i}") for i in range(2)]
        s_decoded = [sem(f"s_decoded{i}") for i in range(2)]
        s_stats = [sem(f"s_stats{i}") for i in range(2)]
        s_std = [sem(f"s_std{i}") for i in range(2)]
        s_norm = [sem(f"s_norm{i}") for i in range(2)]
        s_h = [sem(f"s_h{i}") for i in range(2)]
        s_tp = [sem(f"s_tp{i}") for i in range(2)]
        s_hT = [sem(f"s_hT{i}") for i in range(2)]
        s_hlo = sem("s_hlo")
        s_whi = sem("s_whi")
        s_wlo = sem("s_wlo")
        s_mm = [sem(f"s_mm{i}") for i in range(2)]
        s_staged = [sem(f"s_staged{i}") for i in range(2)]
        s_stored0 = sem("s_stored0")
        s_stored1 = [sem(f"s_stored1_{u}") for u in range(TU)]
        s_bankfree = [sem(f"s_bankfree{i}") for i in range(2)]
        s_agg = [sem(f"s_agg{i}") for i in range(2)]
        s_idx = sem("s_idx")
        s_gather = [sem(f"s_gather{u}") for u in range(U)]
        s_ohm = sem("s_ohm")
        s_ohw = sem("s_ohw")
        s_msg = sem("s_msg")
        s_acc = sem("s_acc")
        s_final = sem("s_final")
        s_out = sem("s_out")
        s_place = sem("s_place")
        s_zero = sem("s_zero")
        s_zeroed = sem("s_zeroed")
        s_pay = sem("s_pay")
        s_payring = sem("s_payring")
        s_scat = [sem(f"s_scat{u}") for u in range(U0)]
        s_back = [sem(f"s_back{i}") for i in range(2)]

        block = ctx.enter_context(nc.Block())

        @block.sync
        def _(sp):
            def edges(a):
                return a.rearrange("(p c) -> p c", p=EP)
            sp.dma_start(dst_i[:, :], edges(dst)).then_inc(s_dst, 16)
            sp.dma_start(src_i[:, :], edges(src)).then_inc(s_edges, 16)
            sp.dma_start(type_i[:, :], edges(etype)).then_inc(s_edges, 16)
            sp.dma_start(ew_f[:, :], edges(ew)).then_inc(s_edges, 16)
            sp.wait_ge(s_zero, 1)
            for i in range(2):
                parts = 4 >> i
                sp.dma_start(scattered[i].rearrange("(p a t) k -> p a (t k)", p=P, a=parts),
                             zeros16[:, :].bitcast(f32).rearrange("p (a t) -> p a t", a=1)
                             .broadcast_to([P, parts, T // 2])).then_inc(s_zeroed, 16)
            sp.wait_ge(s_const, 2)
            sp.dma_start(x_sb[0:NREST, NFULL, :], x[NFULL * P:N, :]).then_inc(s_x, 16)
            sp.dma_start(x_sb[:, 0:NFULL, :],
                         x[0:NFULL * P, :].rearrange("(b p) d -> p b d", p=P)).then_inc(s_x, 16)
            sp.dma_start(w0_sb[:, :, :], w0.rearrange("(k p) d -> p k d", p=P)).then_inc(s_w, 16)
            sp.dma_start(bias0[:, :], b0.partition_broadcast(P)).then_inc(s_bias, 16)
            sp.dma_start(bias1[:, :], b1.partition_broadcast(P)).then_inc(s_bias, 16)
            with sp.Fori(0, NB) as b:
                sp.wait_ge(s_staged[0], b + 1)
                sp.dma_start(table0[ds(b * P, P), :], stage0).then_inc(s_stored0, 16)
            for u in range(U0):
                sp.wait_ge(s_scat[u], 16 * SCAT0)
            sp.dma_start(back, scattered[0].rearrange("(p t) k -> p t k", p=P)).then_inc(s_back[0], 16)
            sp.wait_ge(s_place, 1)
            for k in range(KC):
                sp.dma_start(w1_sb[:, k, :, :],
                             w1[:, k * P:(k + 1) * P, :].rearrange("r p d -> p r d")).then_inc(s_w, 16)
            table1_rows = table1.rearrange("(r n) d -> n r d", r=R)
            def store_block(i, u):
                sp.wait_ge(s_bankfree[1], i * (TU * G1) + (u + 1) * G1)
                sp.dma_start(table1_rows[ds(i * (TU * P) + u * P, P), :, :],
                             stage1[:, u, :, :]).then_inc(s_stored1[u], 16)

            with sp.Fori(0, NB // TU - 1) as i:
                for u in range(TU):
                    store_block(i, u)
            for u in range(TU - 1):
                store_block(NB // TU - 1, u)
            for g in range(G1):
                sp.wait_ge(s_bankfree[1], (NB - 1) * G1 + g + 1)
                sp.dma_start(table1_rows[(NB - 1) * P:NB * P, 2 * g:2 * g + 2, :],
                             stage1[:, TU - 1, 2 * g:2 * g + 2, :]).then_inc(s_stored1[TU - 1], 16)
            for g in range(NB // TU):
                sp.wait_ge(s_final, min((g + 1) * TU, NFULL))
                full = min((g + 1) * TU, NFULL)
                sp.dma_start(out[g * TU * P:full * P, :].rearrange("(b p) d -> p b d", p=P),
                             x1_sb[:, g * TU:full, :]).then_inc(s_out, 16)
            sp.wait_ge(s_final, NB)
            sp.dma_start(out[NFULL * P:N, :], x1_sb[0:NREST, NFULL, :]).then_inc(s_out, 16)
            sp.wait_ge(s_out, 16 * (NB // TU + 1))

        @block.gpsimd
        def _(pool):
            allow = dict(allow_small_or_imprecise_dtypes=True)
            nc.gpsimd.iota(iota_p[:, :], pattern=[[1, P]], base=0, channel_multiplier=0, **allow)
            nc.gpsimd.iota(iota_g16[:, :, :], pattern=[[1, P], [0, G]], base=0, channel_multiplier=0, **allow)
            nc.gpsimd.iota(iota_t16[:, :], pattern=[[1, T]], base=0, channel_multiplier=0, **allow)
            nc.gpsimd.iota(part[:, :], pattern=[[0, 1]], base=0, channel_multiplier=1, **allow)
            nc.gpsimd.memset(zeros16[:, :], 0.0).then_inc(s_zero, 1)
            nc.gpsimd.memset(eps_t[:, :], EPS)
            nc.gpsimd.memset(ones[:, :], 1.0).then_inc(s_const, 1)
            nc.gpsimd.memset(x_sb[:, NFULL, :], 0.0).then_inc(s_const, 1)

            def scatter_columns(layer, i, first):
                fields = pay if layer == 0 else pay1.rearrange("p (c k) -> p c k", k=1)
                places = place if layer == 0 else place1
                width = 2 - layer
                for u in range(U0):
                    if u % G == 0:
                        if not first:
                            for v in range(u, u + G):
                                pool.wait_ge(s_scat[v], i * 16 + layer * 16 * SCAT0)
                        nc.gpsimd.tensor_copy(pay_ring[:, u:u + G, 0:width], fields[:, ds(i * U0 + u, G), :])
                        nc.gpsimd.tensor_copy(place_ring[:, u:u + G],
                                              places[:, ds(i * U0 + u, G)]).then_inc(s_payring, 1)
                        pool.wait_ge(s_payring, i * (U0 // G) + (u // G + 1 + layer * SCAT0 * (U0 // G)))
                        pool.nop(nofuse=True)
                    pool.indirect_dma_start(
                        out=scattered[layer][:, :],
                        out_offset=bass.IndirectOffsetOnAxis(ap=place_ring[:, u:u + 1], axis=0),
                        in_=pay_ring[:, u, 0:width], in_offset=None).then_inc(s_scat[u], 16)

            pool.wait_ge(s_zeroed, 32)
            pool.wait_ge(s_pay, 1)
            scatter_columns(0, 0, True)
            with pool.Fori(1, SCAT0) as i:
                scatter_columns(0, i, False)
            for layer in range(2):
                if layer == 0:
                    pool.wait_ge(s_stored0, 16 * NB)
                else:
                    pool.wait_ge(s_pay, 2)
                    with pool.Fori(0, SCAT1) as i:
                        scatter_columns(1, i, False)
                    for u in range(U0):
                        pool.wait_ge(s_scat[u], 16 * (SCAT0 + SCAT1))
                    pool.wait_ge(s_msg, T)
                    pool.dma_start(back1, scattered[1].rearrange("(p t) k -> p (t k)", p=P)).then_inc(s_back[1], 16)
                    for u in range(TU):
                        pool.wait_ge(s_stored1[u], 16 * (NB // TU + (G1 - 1) * (u == TU - 1)))
                with pool.Fori(0, TI) as i:
                    for u in range(U):
                        if u % RF == 0:
                            pool.wait_ge(s_idx, i * (U // RF) + (u // RF + layer * (T // RF) + 1))
                            pool.nop(nofuse=True)
                        pool.indirect_dma_start(
                            out=rows[:, u, :], out_offset=None, in_=tables[layer][:, :],
                            in_offset=bass.IndirectOffsetOnAxis(ap=idx_ring[:, u:u + 1], axis=0),
                        ).then_inc(s_gather[u], 16)

        @block.scalar
        def _(act):
            act.wait_ge(s_x, 32)
            act.wait_ge(s_const, 2)
            def mean(b):
                nc.scalar.activation(x1_sb[:, ds(b, 1), :], x_sb[:, ds(b, 1), :], ACT.Identity, scale=-1.0 / D,
                                     accum_out=st_mean[:, ds(b, 1)]).then_inc(s_stats[0], 1)

            def deviation(b):
                nc.scalar.activation(x1_sb[:, ds(b, 1), :], x_sb[:, ds(b, 1), :], ACT.Square,
                                     bias=st_mean[:, ds(b, 1)],
                                     accum_out=st_sq[:, ds(b, 1)]).then_inc(s_stats[0], 1)

            mean(0)
            with act.Fori(1, NB) as b:
                mean(b)
            act.wait_ge(s_stats[0], NB)
            deviation(0)
            with act.Fori(1, NB) as b:
                deviation(b)
            act.wait_ge(s_stats[0], 2 * NB)
            nc.scalar.activation(st_std[:, :], st_sq[:, :], ACT.Sqrt, bias=eps_t[:, 0:1],
                                 scale=1.0 / D).then_inc(s_std[0], 1)

            act.wait_ge(s_norm[0], 1)
            def ew_fields(i, u):
                act.wait_ge(s_ohp, i * (U0 // G) + (u // G + 1))
                for v in range(u, u + G):
                    for k in range(2):
                        last = nc.scalar.activation(oh_f[3 + k][:, u // G % FR, :, v % G],
                                                    oh_p[:, u // G % FR, :, v % G], ACT.Copy,
                                                    scale=ew_part[k][:, ds(i * U0 + v, 1)])
                    last.then_inc(s_fieldready, 1)

            act.wait_ge(s_ewpart, 1)

            def table0_block(b, first):
                nc.scalar.activation(h_ring[:, 0, :], x_sb[:, ds(b, 1), :], ACT.Relu, bias=shift[:, ds(b, 1)],
                                     scale=rstd[:, ds(b, 1)]).then_inc(s_h[0], 1)
                ew_fields(b, 0)
                act.wait_ge(s_tp[0], b + 1)
                nc.scalar.activation(hT_ring[:, 0, :, :], bank_h0, ACT.Copy).then_inc(s_hT[0], 1)
                ew_fields(b, G)
                act.wait_ge(s_mm[0], b + 1)
                if not first:
                    act.wait_ge(s_stored0, b * 16)
                nc.scalar.activation(stage0, bank[6][:, 0:D], ACT.Copy).then_inc(s_staged[0], 1)

            table0_block(0, True)
            with act.Fori(1, NB) as b:
                table0_block(b, False)
            for u in range(0, U0, G):
                ew_fields(NB, u)

            def refill(layer, u, t):
                nc.scalar.activation(idx_ring[:, u:u + RF], idx[layer][:, ds(t, RF)], ACT.Copy).then_inc(s_idx, 1)

            def key_fields(i, u):
                act.wait_ge(s_ohp, i * (U // G) + (u // G + 1 + EC0 // G - SORT1.start * (U // G)))
                for v in range(u, u + G):
                    for k, f in enumerate((hi[1], lo[1])):
                        last = nc.scalar.activation(oh_f[k][:, u // G % FR, :, v % G],
                                                    oh_p[:, u // G % FR, :, v % G], ACT.Copy, scale=f[:, ds(i * U + (v - SORT1.start * U), 1)])
                    last.then_inc(s_fieldready, 1)

            def feed(layer, i, last, sort=False):
                for u in range(U):
                    if sort and u % G == 0:
                        key_fields(i, u + G)
                    if layer == 0 and not (last and u + AHEAD >= U):
                        if u % AHEAD == 0:
                            act.wait_ge(s_ohm, i * (U // AHEAD) + (u // AHEAD + 2))
                        scaled((u + AHEAD) % U, i * U + (u + AHEAD))
                    if u % RF == RF - 1 and not last:
                        act.wait_ge(s_msg, i * U + (u + 1 + layer * T))
                        refill(layer, u + 1 - RF, i * U + (u + 1 - RF + U))

            def scaled(u, t):
                nc.scalar.activation(oh_m[:, u, :], oh_m[:, u, :], ACT.Copy,
                                     scale=ew_s[:, ds(t, 1)]).then_inc(s_ohw, 1)

            def std_part(n, part):
                act.wait_ge(s_stats[1], n)
                nc.scalar.activation(st_std[:, part], st_sq[:, part], ACT.Sqrt, bias=eps_t[:, 0:1],
                                     scale=1.0 / D).then_inc(s_std[1], 1)

            for layer in range(2):
                if layer == 1:
                    def hidden(u, b):
                        nc.scalar.activation(h_ring[:, u, :], x1_sb[:, ds(b, 1), :], ACT.Relu,
                                             bias=shift[:, ds(b, 1)], scale=rstd[:, ds(b, 1)]).then_inc(s_h[1], 1)

                    def high_part(i, u):
                        act.wait_ge(s_tp[1], i * TU + (u + 1))
                        nc.scalar.activation(hT_hi[:, u, :, :], transposed(u), ACT.Copy).then_inc(s_hT[1], 1)

                    act.wait_ge(s_norm[1], 1)
                    for u in range(TU):
                        hidden(u, u)
                    for u in range(TU):
                        high_part(0, u)
                    std_part(2, slice(TU, NB))
                    act.wait_ge(s_norm[1], 2)
                    for u in range(TU):
                        hidden(u, TU + u)

                    def hidden_group(i, last):
                        for u in range(TU):
                            act.wait_ge(s_mm[1], i * (TU * G1) + (u + 1 - TU) * G1)
                            high_part(i, u)
                            if not last:
                                hidden(u, i * TU + (u + TU))

                    with act.Fori(1, NB // TU - 1) as i:
                        hidden_group(i, False)
                    hidden_group(NB // TU - 1, True)
                act.wait_ge(s_index[layer], 1)
                if layer == 1:
                    act.wait_ge(s_msg, T)
                for u in range(0, U, RF):
                    if layer == 0 and u == U - RF:
                        act.wait_ge(s_decoded[0], 1)
                    refill(layer, u, u)
                if layer == 0:
                    act.wait_ge(s_ohm, 1)
                    for u in range(AHEAD):
                        scaled(u, u)
                    act.wait_ge(s_x1, NB)
                    nc.scalar.activation(agg1[:, :, :], bias1[:, :].rearrange("p (b d) -> p b d", b=1)
                                         .broadcast_to([P, NB, D]), ACT.Copy).then_inc(s_agginit, 1)
                if layer == 0:
                    feed(0, 0, False)
                    key_fields(SORT1.start, 0)
                    with act.Fori(SORT1.start, SORT1.stop) as i:
                        feed(0, i, False, True)
                    feed(0, SORT1.stop, False)
                    act.wait_ge(s_w, 16 * (1 + KC))
                    act.wait_ge(s_sorted[1], 1)
                    act.wait_ge(s_pay, 2)
                    for k in range(KC):
                        nc.scalar.activation(w1_hi[:, k, :, :], w1_sb[:, k, :, :], ACT.Copy).then_inc(s_whi, 1)
                with act.Fori(0 if layer else SORT1.stop + 1, TI - 1) as i:
                    feed(layer, i, False)
                if layer == 0:
                    std_part(1, slice(0, TU))
                feed(layer, TI - 1, True)

        @block.vector
        def _(dve):
            steps = [0]

            def step(ins):
                steps[0] += 1
                ins.then_inc(s_dve, 1)
                dve.wait_ge(s_dve, steps[0])

            V = nc.vector
            dve.sem_inc(s_acc, 1)
            dve.wait_ge(s_const, 1)
            V.tensor_scalar(before[:, :], iota_p[:, :], part[:, 0:1], None, ALU.is_gt)
            V.tensor_scalar(upto[:, :], iota_p[0:NB, 0:NB], part[0:NB, 0:1], None, ALU.is_ge)
            step(V.tensor_scalar(ident[:, :], iota_p[:, :], part[:, 0:1], None, ALU.is_equal))
            V.sem_inc(s_ident, 1)

            def buckets(layer):
                node = dst_i if layer == 0 else src_i
                step(V.tensor_scalar(tmp_i[:, :], node[:, :], 7, None, ALU.logical_shift_right))
                step(V.tensor_copy(bucket[:, :], tmp_i[:, :]))

            def keys(layer):
                key_hi = pos_t[layer]
                node, other = (dst_i, src_i) if layer == 0 else (src_i, dst_i)
                step(V.tensor_scalar(tmp_i[:, :], node[:, :], P - 1, None, ALU.bitwise_and))
                step(V.tensor_copy(key_lo[:, :], tmp_i[:, :]))
                if layer == 0:
                    step(V.tensor_copy(row_f[:, :], other[:, :]))
                else:
                    step(V.tensor_copy(row_f[:, :], type_i[:, :]))
                    step(V.tensor_copy(tmp_f[:, :], other[:, :]))
                    step(V.scalar_tensor_tensor(row_f[:, :], row_f[:, :], float(NP), tmp_f[:, :],
                                                ALU.mult, ALU.add))
                step(V.tensor_copy(tmp_i[:, :], row_f[:, :]))
                step(V.tensor_scalar(tmp_i[:, :], tmp_i[:, :], 4, None, ALU.logical_shift_right))
                step(V.tensor_copy(key_hi[:, :], tmp_i[:, :]))
                step(V.scalar_tensor_tensor(tmp_f[:, :], key_hi[:, :], -float(KEY_LOW), row_f[:, :],
                                            ALU.mult, ALU.add))
                step(V.tensor_scalar(hi[layer][:, :], key_hi[:, :], 1.0, None, ALU.add))
                step(V.scalar_tensor_tensor(lo[layer][:, :], tmp_f[:, :], float(P), key_lo[:, :],
                                            ALU.mult, ALU.add))

            def masks(b):
                return V.tensor_scalar(mask[:, ds(b, 1), :], bucket[:, :], b_col(b), None, ALU.is_equal)

            def row_totals(layer):
                V.tensor_copy(row_tot[:, :], scan3[:, :, EC - 1]).then_inc(s_rowtot[layer], 1)

            def block_offsets(layer):
                dve.wait_ge(s_total[layer], 1)
                step(V.tensor_scalar(tiles_f[:, :], RANK[:, 0:NB], float(P - 1), None, ALU.add))
                step(V.tensor_copy(tot_i[:, :], tiles_f[:, :]))
                step(V.tensor_scalar(tot_i[:, :], tot_i[:, :], 7, None, ALU.logical_shift_right))
                step(V.tensor_copy(tiles_f[:, :], tot_i[:, :]))
                step(V.tensor_tensor_scan(tile_end[:, :], tiles_f[:, :], tiles_f[:, :], 0.0,
                                          ALU.add, ALU.max))
                step(V.tensor_tensor(tile_end[:, :], tile_end[:, :], tiles_f[:, :], ALU.subtract))
                step(V.tensor_scalar(tile_end[:, :], tile_end[:, :], float(P), -1.0, ALU.mult, ALU.add))
                step(V.tensor_tensor(offs[0:EP, :], tile_end[0:EP, :], RANK[0:EP, 32:32 + NB], ALU.add))

            def tile_counts(layer):
                step(V.tensor_scalar(col_f[:, :], column(layer, 0), float(P - 1), None, ALU.add))
                step(V.tensor_copy(col_i[:, :], col_f[:, :]))
                step(V.tensor_scalar(col_i[:, :], col_i[:, :], 7, None, ALU.logical_shift_right))
                V.tensor_copy(col_f[:, :], col_i[:, :]).then_inc(s_colend[layer], 1)

            def ended_blocks(layer):
                dve.wait_ge(s_colcum[layer], 1)
                step(V.tensor_copy(col_end[:, :], column(layer, 1)))
                V.tensor_scalar(ended, iota_t16[0:NB, :], col_end[:, 0:1], None,
                                ALU.is_ge).then_inc(s_ended[layer], 1)

            def tile_offsets(layer):
                dve.wait_ge(s_tilerow[layer], 1)
                step(V.tensor_scalar(tile_off[layer][:, :], RANK[0:1, 0:T], float(NB - 1), float(D),
                                     ALU.min, ALU.mult))

            def place_block(b):
                return V.scalar_tensor_tensor(scan3[:, ds(b, 1), :], scan3[:, ds(b, 1), :], offs[0:EP, ds(b, 1)],
                                              mask[:, ds(b, 1), :], ALU.add, ALU.mult)

            def positions(layer):
                dve.wait_ge(s_possum[layer], 1)
                step(V.tensor_copy(tmp_i[:, :], RANK[0:EP, 0:EC]))
                step(V.tensor_scalar(tmp_i[:, :], tmp_i[:, :], 7, None, ALU.logical_shift_right))
                step(V.tensor_copy(pos_t[layer][:, :], tmp_i[:, :]))
                step(V.scalar_tensor_tensor(pos_p[layer][:, :], pos_t[layer][:, :], -float(P), RANK[0:EP, 0:EC],
                                            ALU.mult, ALU.add))

            b_tab = iota_p

            def b_col(b):
                return b_tab[0:EP, ds(b, 1)]

            def scan_block(b):
                m = mask[:, ds(b, 1), :].rearrange("p a c -> p (a c)")
                s = scan3[:, ds(b, 1), :].rearrange("p a c -> p (a c)")
                return V.tensor_tensor_scan(s, m, m, 0.0, ALU.add, ALU.max)

            def sort_fields(layer, i, u):
                step_cols, c0 = (U, SORT1.start * U) if layer else (U0, 0)
                c = i * step_cols + (u - c0)
                r = u // G % FR
                dve.wait_ge(s_sortfree, c + (SR - G + layer * EC0))
                own = [EP, P, G]
                def cols(a):
                    return a[:, ds(c, G)].rearrange("p (m g) -> p m g", m=1).broadcast_to(own)
                V.tensor_tensor(oh_p[:, r, :, :], iota_g16[0:EP, :, :], cols(pos_p[layer]),
                                ALU.is_equal).then_inc(s_ohp, 1)
                dve.wait_ge(s_ohp, i * (step_cols // G) + (u // G + 1 + (layer * EC0 - c0) // G))
                if layer == 0:
                    for k, f in enumerate((hi[0], lo[0], ew16_0)):
                        V.tensor_tensor(oh_f[k][:, r, :, :], oh_p[:, r, :, :], cols(f), ALU.mult)

            def sort_tile(layer, c, u):
                V.tensor_scalar(oh_t[:, u % SR, :], iota_t16[0:EP, :], pos_t[layer][:, ds(c, 1)], None,
                                ALU.is_equal).then_inc(s_sortready, 1)

            def hold_keys(layer):
                dve.wait_ge(s_sorted[layer], 1)
                part_hi = free0[:, 3 * T:4 * T] if layer == 0 else scan[:, 0:T]
                key = free0[:, 2 * T:3 * T] if layer == 0 else key_hold
                step(V.tensor_copy(part_hi, bank[0][:, 0:T]))
                step(V.scalar_tensor_tensor(key, part_hi, float(KEY_LOW * P), bank[1][:, 0:T],
                                            ALU.mult, ALU.add))

            def decode(layer):
                if layer == 0:
                    hold_keys(0)
                dec_i, dec_j = (free0[:, k * T:(k + 1) * T].bitcast(i32) for k in (0, 1))
                dec_f, dec_g = (free0[:, k * T:(k + 1) * T] for k in (2, 3))
                dve.wait_ge(s_back[layer], 16)
                if layer == 0:
                    step(V.tensor_tensor(dec_f, dec_f, back[:, :, 0], ALU.add))
                else:
                    step(V.tensor_tensor(dec_f, key_hold, back1, ALU.add))
                step(V.tensor_copy(dec_i, dec_f))
                step(V.tensor_scalar(dec_j, dec_i, 7, None, ALU.logical_shift_right))
                V.tensor_scalar(idx[layer][:, :], dec_j, -float(KEY_LOW), 0.0, ALU.add,
                                ALU.max).then_inc(s_index[layer], 1)
                step(V.tensor_scalar(dec_g.bitcast(i32), dec_i, P - 1, None, ALU.bitwise_and))
                step(V.tensor_copy(local[layer][:, :], dec_g.bitcast(i32)))
                step(V.tensor_scalar(dec_g, dec_f, 0.0, -2.0 * P, ALU.is_equal, ALU.mult))
                step(V.tensor_tensor(local[layer][:, :], local[layer][:, :], dec_g, ALU.add))
                if layer == 0:
                    step(V.tensor_copy(dec_g, bank[2][:, 0:T]))
                    step(V.tensor_tensor(dec_g, dec_g, bank[3][:, 0:T], ALU.add))
                    step(V.tensor_tensor(dec_g, dec_g, bank[4][:, 0:T], ALU.add))
                    step(V.tensor_tensor(ew_s[:, :], dec_g, back[:, :, 1], ALU.add))
                V.sem_inc(s_decoded[layer], 1)

            def one_hots(layer, t, u):
                own = [P, AHEAD, P]
                V.tensor_tensor(oh_m[:, u:u + AHEAD, :],
                                iota_p[:, :].rearrange("p (a m) -> p a m", a=1).broadcast_to(own),
                                local[layer][:, ds(t, AHEAD)].rearrange("p (a m) -> p a m", m=1).broadcast_to(own),
                                ALU.is_equal).then_inc(s_ohm, 1)

            dve.wait_ge(s_dst, 16)
            buckets(0)
            with dve.Fori(0, NB // TU) as i:
                for u in range(TU):
                    masks(i * TU + u).then_inc(s_mask, 1)
                for u in range(TU):
                    dve.wait_ge(s_mask, i * TU + (u + 1))
                    scan_block(i * TU + u).then_inc(s_scan, 1)
            dve.wait_ge(s_scan, NB)
            row_totals(0)
            block_offsets(0)
            with dve.Fori(0, NB // TU) as i:
                for u in range(TU):
                    place_block(i * TU + u).then_inc(s_placed, 1)
            tile_counts(0)
            dve.wait_ge(s_edges, 48)
            keys(0)
            step(V.tensor_copy(ew16_0[:, :], ew_f[:, 0:EC0]))
            step(V.tensor_tensor(tmp_f[:, 0:EC0], ew_f[:, 0:EC0], ew16_0[:, :], ALU.subtract))
            step(V.tensor_copy(ew16[:, :], tmp_f[:, 0:EC0]))
            V.tensor_copy(ew_part[0][:, :], ew16[:, :])
            V.tensor_tensor(ew_part[1][:, :], tmp_f[:, 0:EC0], ew16[:, :], ALU.subtract).then_inc(s_ewpart, 1)
            own = slice(EC0, EC)
            step(V.scalar_tensor_tensor(pay[:, :, 0], hi[0][:, own], float(KEY_LOW * P), lo[0][:, own],
                                        ALU.mult, ALU.add))
            step(V.tensor_copy(pay[:, :, 1], ew_f[:, own]))
            positions(0)
            step(V.scalar_tensor_tensor(place, pos_p[0][:, own], float(T), pos_t[0][:, own], ALU.mult, ALU.add))
            V.sem_inc(s_pay, 1)

            def sort_group(i):
                for u in range(U0):
                    if u % G == 0:
                        sort_fields(0, i, u)
                    sort_tile(0, i * U0 + u, u)

            def rank_block(b):
                masks(b).then_inc(s_mask, 1)
                dve.wait_ge(s_mask, b + (NB + 1))
                scan_block(b).then_inc(s_scan, 1)

            def init_block(b):
                V.tensor_tensor(x1_sb[:, ds(b, 1), :], x_sb[:, ds(b, 1), :],
                                bias0[:, :].rearrange("p (b d) -> p b d", b=1), ALU.add).then_inc(s_x1, 1)

            ended_blocks(0)

            dve.wait_ge(s_std[0], 1)
            step(V.reciprocal(rstd[:, :], st_std[:, :]))
            step(V.tensor_tensor(shift[:, :], st_mean[:, :], rstd[:, :], ALU.mult))
            V.sem_inc(s_norm[0], 1)
            sort_group(0)
            tile_offsets(0)
            buckets(1)
            rank_block(0)
            dve.wait_ge(s_bias, 32)
            init_block(0)
            with dve.Fori(1, HALF) as i:
                sort_group(i)
                rank_block(i * 2 - 1)
                rank_block(i * 2)
                init_block(i)
            dve.wait_ge(s_scan, 2 * NB)
            row_totals(1)

            def place_blocks(i):
                for k in range(2):
                    place_block(i * 2 + (k - 2 * HALF)).then_inc(s_placed, 1)
                init_block(i)

            sort_group(HALF)
            block_offsets(1)
            tile_counts(1)
            place_blocks(HALF)
            sort_group(HALF + 1)
            ended_blocks(1)
            place_blocks(HALF + 1)
            with dve.Fori(HALF + 2, NB) as i:
                sort_group(i)
                place_blocks(i)
            tile_offsets(1)
            place_block(NB - 1).then_inc(s_placed, 1)
            sort_group(NB)
            keys(1)
            decode(0)
            one_hots(0, 0, 0)
            dve.wait_ge(s_x1, NB)

            def offsets(layer, t):
                _, offs = nc.values_load_multi_w_load_instructions(
                    tile_off[layer][0:1, ds(t, LAG)], engines=[mybir.EngineType.DVE], min_val=0,
                    max_val=(NB - 1) * D, skip_runtime_bounds_check_because="tile_offsets() clamps them")
                return offs

            def accumulate(layer, off, u, n):
                acc = (x1_sb if layer == 0 else agg1)[:, :, :].rearrange("p b d -> p (b d)")
                dve.wait_ge(s_acc, n + 1)
                V.tensor_tensor(acc[:, ds(off, D)], acc[:, ds(off, D)], message_bank(u), ALU.add).then_inc(s_acc, 1)

            def message_group(layer, i, first, last, sort, summed=None):
                for u in range(U):
                    if u % LAG == 0 and (u >= LAG or not first):
                        offs = offsets(layer, i * U + (u - LAG))
                    if u % 2 == 0 and (u >= LAG or not first):
                        dve.wait_ge(s_msg, i * U + (u - LAG + layer * T + 2))
                    if sort and u % G == G // 2:
                        sort_fields(1, i, u + G // 2)
                    if sort:
                        sort_tile(1, i * U + (u - SORT1.start * U), u)
                    if u % AHEAD == LAG and not (last and u + AHEAD > U):
                        one_hots(layer, i * U + (u + AHEAD - LAG), (u + AHEAD - LAG) % U)
                    if u >= LAG or not first:
                        accumulate(layer, offs[u % LAG], (u - LAG) % U, i * U + (u - LAG + layer * T))
                        if summed:
                            summed(i * U + (u - LAG + 1))
                if last:
                    offs = offsets(layer, i * U + (U - LAG))
                    for u in range(U - LAG, U):
                        if u % 2 == 0:
                            dve.wait_ge(s_msg, i * U + (u + 2 + layer * T))
                        accumulate(layer, offs[u % LAG], u, i * U + (u + layer * T))
                        if summed:
                            summed(i * U + u + 1)

            message_group(0, 0, True, False, False)
            positions(1)
            V.sem_inc(s_place, 1)
            own1 = slice(EC1, EC)
            step(V.scalar_tensor_tensor(pay1, hi[1][:, own1], float(KEY_LOW * P), lo[1][:, own1],
                                        ALU.mult, ALU.add))
            step(V.scalar_tensor_tensor(place1, pos_p[1][:, own1], float(T), pos_t[1][:, own1],
                                        ALU.mult, ALU.add))
            V.sem_inc(s_pay, 1)
            sort_fields(1, SORT1.start, 0)
            with dve.Fori(SORT1.start, SORT1.stop) as i:
                message_group(0, i, False, False, True)
            hold_keys(1)
            with dve.Fori(SORT1.stop, TI - 3) as i:
                message_group(0, i, False, False, False)
            def stats(b):
                V.bn_stats(bn6[:, b, :], x1_sb[:, b, :]).then_inc(s_agg[0], 1)

            for k in range(KC):
                message_group(0, TI - 3 + k, False, False, False)
                dve.wait_ge(s_whi, k + 1)
                V.tensor_tensor(w1_lo[:, k, :, :], w1_sb[:, k, :, :], w1_hi[:, k, :, :].bitcast(f32),
                                ALU.subtract).then_inc(s_wlo, 1)
            def mean_and_var(part):
                dve.wait_ge(s_agg[0], part.stop)
                V.tensor_tensor(st_mean[:, part], bn6[:, part, 1], bn6[:, part, 4], ALU.add)
                V.tensor_tensor(st_sq[:, part], bn6[:, part, 2], bn6[:, part, 5], ALU.add)
                step(V.tensor_tensor(st_sum[:, part], bn6[:, part, 1], bn6[:, part, 4], ALU.subtract))
                step(V.tensor_tensor(st_sum[:, part], st_sum[:, part], st_sum[:, part], ALU.mult))
                V.scalar_tensor_tensor(st_sq[:, part], st_sum[:, part], D / 4.0, st_sq[:, part],
                                       ALU.mult, ALU.add).then_inc(s_stats[1], 1)

            def scale_and_shift(n, part):
                dve.wait_ge(s_std[1], n)
                step(V.reciprocal(rstd[:, part], st_std[:, part]))
                V.scalar_tensor_tensor(shift[:, part], st_mean[:, part], -0.5, rstd[:, part],
                                       ALU.mult, ALU.mult).then_inc(s_norm[1], 1)

            def low_part(i, u):
                dve.wait_ge(s_hT[1], i * TU + (u + 1))
                V.tensor_tensor(hT_lo[:, u, :, :], transposed(u), hT_hi[:, u, :, :].bitcast(f32),
                                ALU.subtract).then_inc(s_hlo, 1)

            first, others = slice(0, TU), slice(TU, NB)

            def norm(t):
                for b in range(NB):
                    if DONE[b] == t:
                        if t == T:
                            dve.wait_ge(s_acc, T + 1)
                        stats(b)
                        if b == TU - 1:
                            mean_and_var(first)
                if t == (TI - 1) * U:
                    scale_and_shift(1, first)

            for t in range(DONE[0], (TI - 1) * U - LAG + 1):
                norm(t)
            message_group(0, TI - 1, False, True, False, norm)
            for u in range(TU):
                low_part(0, u)
            mean_and_var(others)
            scale_and_shift(2, others)


            def stage_group(i, first, last=False):
                for u in range(TU):
                    if not first:
                        dve.wait_ge(s_stored1[u], i * 16)
                    for g in range(G1):
                        dve.wait_ge(s_mm[1], i * (TU * G1) + (u * G1 + g + 1))
                        V.tensor_copy(stage1[:, u, 2 * g:2 * g + 2, :].rearrange("p r d -> p (r d)"),
                                      table_bank(g)[:, :]).then_inc(s_bankfree[1], 1)
                    if not last:
                        low_part(i + 1, u)

            stage_group(0, True)
            with dve.Fori(1, NB // TU - 1) as i:
                stage_group(i, False)
            decode(1)
            stage_group(NB // TU - 1, False, True)
            dve.wait_ge(s_agginit, 1)

            one_hots(1, 0, 0)
            message_group(1, 0, True, False, False)
            with dve.Fori(1, TI - 1) as i:
                message_group(1, i, False, False, False)
            def output(t):
                for b in range(NB):
                    if DONE[b] == t:
                        if t == T:
                            dve.wait_ge(s_acc, 2 * T + 1)
                        V.scalar_tensor_tensor(x1_sb[:, b, :], agg1[:, b, :], 0.0, x1_sb[:, b, :],
                                               ALU.max, ALU.add).then_inc(s_final, 1)

            for t in range(DONE[0], (TI - 1) * U - LAG + 1):
                output(t)
            message_group(1, TI - 1, False, True, False, output)

        @block.tensor
        def _(pe):
            TE = nc.tensor
            pe.sem_inc(s_sortfree, SR)

            def rank_products(layer):
                if layer == 0:
                    pe.wait_ge(s_const, 1)
                    pe.wait_ge(s_ident, 1)
                pe.wait_ge(s_rowtot[layer], 1)
                kw = dict(start=True, stop=True)
                TE.matmul(RANK[:, 0:NB], ones[0:EP, :], row_tot[:, :], **kw)
                TE.matmul(RANK[:, 32:32 + NB], before[0:EP, :], row_tot[:, :], **kw)
                TE.matmul(column(layer, 0), row_tot[:, :], ones[0:EP, 0:1], **kw).then_inc(s_total[layer], 1)

            def through_block(layer):
                pe.wait_ge(s_colend[layer], 1)
                TE.matmul(column(layer, 1), upto[:, :], col_f[:, :], start=True,
                          stop=True).then_inc(s_colcum[layer], 1)

            def count_ended(layer):
                pe.wait_ge(s_ended[layer], 1)
                TE.matmul(RANK[0:1, 0:T], ones[0:NB, 0:1], ended, start=True,
                          stop=True).then_inc(s_tilerow[layer], 1)

            def sum_places(layer):
                own = (slice(0, EP), slice(0, EC))
                pe.wait_ge(s_placed, 2 * NB if layer else 1)
                TE.matmul(RANK[own], zeros16[0:EP, 0:EP], zeros16[own], start=True, stop=False)
                with pe.Fori(0, NB // TU) as i:
                    for u in range(TU):
                        b = i * TU + u
                        if layer == 0:
                            pe.wait_ge(s_placed, b + 1)
                        TE.matmul(RANK[own], ident[0:EP, 0:EP], scan3[:, ds(b, 1), :], start=False, stop=False)
                TE.matmul(RANK[own], zeros16[0:EP, 0:EP], zeros16[own],
                          start=False, stop=True).then_inc(s_possum[layer], 1)

            def transposes(i, u, first):
                pe.wait_ge(s_h[1], i * TU + (u + 1))
                if u == TU - 1 or not first:
                    pe.wait_ge(s_hlo, i * TU + (1 if u == TU - 1 else 0 if u == 0 else u + 1 - TU))
                for k in range(KC):
                    last = TE.transpose(transposed(u)[:, k, :], h_ring[:, u, k * P:(k + 1) * P], ident[:, :])
                last.then_inc(s_tp[1], 1)

            def table_rows(i, u, first):
                pe.wait_ge(s_hlo, i * TU + (u + 1))
                for g in range(G1):
                    if not (first and u == 0):
                        pe.wait_ge(s_bankfree[1], i * (TU * G1) + (u * G1 + g + 1 - G1))
                    for k in range(KC):
                        for j, (h, w) in enumerate(((hT_hi, w1_hi), (hT_hi, w1_lo), (hT_lo, w1_hi))):
                            last = TE.matmul(table_bank(g)[:, :], h[:, u, k, :],
                                             w[:, k, 2 * g:2 * g + 2, :].rearrange("p r d -> p (r d)"),
                                             start=(k + j == 0), stop=(k == KC - 1 and j == 2))
                    last.then_inc(s_mm[1], 1)

            def table():
                pe.wait_ge(s_wlo, KC)
                for u in range(TU):
                    transposes(0, u, True)
                for u in range(TU):
                    table_rows(0, u, True)
                    transposes(1, u, False)
                with pe.Fori(1, NB // TU - 1) as i:
                    for u in range(TU):
                        table_rows(i, u, False)
                        transposes(i + 1, u, False)
                for u in range(TU):
                    table_rows(NB // TU - 1, u, False)

            def sort_edges(layer, kind):
                for k in range(NSF[layer]):
                    last = TE.matmul(bank[k][:, 0:T], zeros16[0:EP, 0:P], zeros16[0:EP, :],
                                     start=(kind == "open"), stop=(kind == "close"))
                if kind == "close":
                    last.then_inc(s_sorted[layer], 1)

            def sort_tile(layer, u, n1):
                pe.wait_ge(s_fieldready, n1)
                pe.wait_ge(s_sortready, n1)
                for k in range(NSF[layer]):
                    last = TE.matmul(bank[k][:, 0:T], oh_f[k][:, u // G % FR, :, u % G], oh_t[:, u % SR, :],
                                     start=False, stop=False)
                last.then_inc(s_sortfree, 1)

            def message(layer, i, u, first):
                n1 = i * U + (u + 1 + layer * T)
                if layer == 0:
                    pe.wait_ge(s_ohw, n1)
                else:
                    pe.wait_ge(s_ohm, i * (U // AHEAD) + (u // AHEAD + 1 + T // AHEAD))
                pe.wait_ge(s_gather[u], i * 16 + 16 * (1 + layer * TI))
                if u % 2 == 0 and not (first and u < RING and layer == 0):
                    pe.wait_ge(s_acc, i * U + (u + 3 - RING + layer * T))
                TE.matmul(message_bank(u), oh_m[:, u, :], rows[:, u, :],
                          start=True, stop=True).then_inc(s_msg, 1)

            rank_products(0)
            pe.wait_ge(s_zero, 1)
            sum_places(0)
            through_block(0)
            pe.wait_ge(s_w, 16)
            sort_edges(0, "open")
            count_ended(0)
            def sort_group(i, block=True):
                for u in range(U0):
                    sort_tile(0, u, i * U0 + (u + 1))
                    if block and u == 1:
                        pe.wait_ge(s_h[0], i + 1)
                        for k in range(KC):
                            last = TE.transpose(bank_h0[:, k, :], h_ring[:, 0, k * P:(k + 1) * P],
                                                ident[:, :])
                        last.then_inc(s_tp[0], 1)
                    if block and u == 4:
                        pe.wait_ge(s_hT[0], i + 1)
                        for k in range(KC):
                            last = TE.matmul(bank[6][:, 0:D], hT_ring[:, 0, k, :], w0_sb[:, k, :],
                                             start=(k == 0), stop=(k == KC - 1))
                        last.then_inc(s_mm[0], 1)

            with pe.Fori(0, HALF) as i:
                sort_group(i)
            rank_products(1)
            sort_group(HALF)
            through_block(1)
            sort_group(HALF + 1)
            count_ended(1)
            with pe.Fori(HALF + 2, NB) as i:
                sort_group(i)
            sort_group(NB, False)
            sort_edges(0, "close")
            sum_places(1)
            pe.wait_ge(s_decoded[0], 1)
            sort_edges(1, "open")

            def group(layer, i, first, sort):
                for u in range(U):
                    message(layer, i, u, first)
                    if sort:
                        sort_tile(1, u, i * U + (EC0 + u + 1 - SORT1.start * U))

            group(0, 0, True, False)
            with pe.Fori(SORT1.start, SORT1.stop) as i:
                group(0, i, False, True)
            sort_edges(1, "close")
            with pe.Fori(SORT1.stop, TI) as i:
                group(0, i, False, False)
            table()
            group(1, 0, True, False)
            with pe.Fori(1, TI) as i:
                group(1, i, False, False)


_INS = ['x', 'src', 'dst', 'edge_type_8', 'edge_weight', 'L0_gnn_weight', 'L0_gnn_bias', 'L1_gnn_weight', 'L1_gnn_bias']
_OUTS = [((3125, 256), 'float32')]


def kernel(**inputs):
    import numpy as _np
    import concourse.bacc as _bacc
    from concourse import mybir as _mybir
    from concourse.bass_utils import run_bass_kernel_spmd as _run

    nc = _bacc.Bacc("TRN2", target_bir_lowering=False, num_devices=1)
    arrays, args = {}, []
    for name in _INS:
        a = _np.ascontiguousarray(inputs[name])
        arrays[f"in_{name}_dram"] = a
        args.append(nc.dram_tensor(f"in_{name}_dram", a.shape, _mybir.dt.from_np(a.dtype), kind="ExternalInput").ap())
    for i, (shape, dtype) in enumerate(_OUTS):
        dt = _mybir.dt.from_np(_np.dtype(dtype))
        args.append(nc.dram_tensor(f"out_{i}_dram", shape, dt, kind="ExternalOutput").ap())
    gnn_kernel(nc, *args)
    r = _run(nc, [arrays], core_ids=[0])
    return r.results[0]["out_0_dram"]
```
